# Optimizing a Trainium2 kernel written in Bass

```python
import numpy as np
import jax
import jax.numpy as jnp

def _softmax(x, axis=-1):
    return jax.nn.softmax(x, axis=axis)

def _gelu(x):
    return jax.nn.gelu(x, approximate=True)

def _silu(x):
    return jax.nn.silu(x)

def _sigmoid(x):
    return jax.nn.sigmoid(x)

def _layernorm(x, axis=-1, eps=1e-05):
    m = jnp.mean(x, axis=axis, keepdims=True)
    v = jnp.var(x, axis=axis, keepdims=True)
    return (x - m) / jnp.sqrt(v + eps)

def _scatter_add(tgt, idx, src, axis=0):
    return tgt.at[idx].add(src)

def _segment_sum(src, seg, n):
    return jax.ops.segment_sum(src, seg, n)
kernel_name = 'mk_perceiver_d1_seqx_r2_0d6eca'

def setup_inputs(seed: int=0):
    np.random.seed(seed)
    _w = jnp.asarray

    def _rec_inputs():
        import jax
        import jax.numpy as jnp
        _rk = jax.random.key(seed)
        x = 7.22e-05 + 1 * jax.random.normal(jax.random.fold_in(_rk, 1), (1, 256, 512), jnp.float32)
        _lenS = 256 - jax.random.randint(jax.random.fold_in(_rk, 7), (1,), 0, max(1, 256 // 4) + 1, jnp.int32)
        _lenS2 = 25088 - jax.random.randint(jax.random.fold_in(_rk, 8), (1,), 0, max(1, 25088 // 4) + 1, jnp.int32)
        _ctx_1024P = jax.random.normal(jax.random.fold_in(_rk, 11), (1, 16, 512), jnp.float32)
        _ctx_1024c = jax.random.dirichlet(jax.random.fold_in(_rk, 511), 0.3 * jnp.ones((16,), jnp.float32), (1, 25088))
        _ctx_1024t = jnp.einsum('bsk,bkd->bsd', _ctx_1024c, _ctx_1024P)
        _ctx_1024t = _ctx_1024t * jax.lax.rsqrt(jnp.mean(jnp.square(_ctx_1024t)) + 1e-12) * 0.953939
        ctx_1024 = 4.13588e-05 + 0.999923 * (_ctx_1024t + 0.3 * jax.random.normal(jax.random.fold_in(_rk, 611), (1, 25088, 512), jnp.float32))
        return (x, ctx_1024)
    x, ctx_1024 = _rec_inputs()

    def _L0_xattn_setup():
        import jax, jax.numpy as jnp
        import numpy as np
        H = 16
        DK = 64
        D_MODEL = 512
        key = jax.random.key(seed)
        ks = jax.random.split(key, 9)
        B, T, D = (4, 1024, D_MODEL)
        scale = 1.0 / np.sqrt(D)
        return {'Q': jax.random.normal(ks[0], (B, T, D), dtype=jnp.float32), 'K': jax.random.normal(ks[1], (B, T, D), dtype=jnp.float32), 'V': jax.random.normal(ks[2], (B, T, D), dtype=jnp.float32), 'Wq': jax.random.normal(ks[3], (D, D), dtype=jnp.float32) * scale, 'bq': jax.random.normal(ks[4], (D,), dtype=jnp.float32) * scale, 'Wk': jax.random.normal(ks[5], (D, D), dtype=jnp.float32) * scale, 'bk': jax.random.normal(ks[6], (D,), dtype=jnp.float32) * scale, 'Wv': jax.random.normal(ks[7], (D, D), dtype=jnp.float32) * scale, 'bv': jax.random.normal(ks[8], (D,), dtype=jnp.float32) * scale}
    _L0_xattn_all = _L0_xattn_setup()
    _L0_xattn_in = {k: v for k, v in _L0_xattn_all.items() if k in ('Wq', 'bq', 'Wk', 'bk', 'Wv', 'bv')}
    del _L0_xattn_all

    def _L0_attn_setup():
        import jax, jax.numpy as jnp
        import numpy as np
        B, L, D = (2, 1024, 512)
        H, K = (16, 16)
        HD = D // H

        def tisa_bias(offsets, amplitudes, sharpness, seq_len):
            rel = jnp.arange(-(seq_len - 1), seq_len, dtype=jnp.float32)
            diff = offsets[:, :, None] - rel[None, None, :]
            scores = jnp.sum(amplitudes[:, :, None] * jnp.exp(-jnp.abs(sharpness)[:, :, None] * diff * diff), axis=1)
            i = jnp.arange(seq_len)
            idx = i[:, None] - i[None, :] + (seq_len - 1)
            return scores[:, idx]
        key = jax.random.key(seed)
        k1, k2, k3, k4, k5 = jax.random.split(key, 5)
        x = jax.random.normal(k1, (B, L, D), dtype=jnp.float32)
        w_in = jax.random.normal(k2, (3 * D, D), dtype=jnp.float32) * 0.02
        kernel_offsets = jax.random.normal(k3, (H, K), dtype=jnp.float32) * 20.0
        kernel_amplitudes = 0.1 + 0.01 * jax.random.normal(k4, (H, K), dtype=jnp.float32)
        kernel_sharpness = 0.1 + 0.01 * jax.random.normal(k5, (H, K), dtype=jnp.float32)
        return {'x': x, 'w_in': w_in, 'kernel_offsets': kernel_offsets, 'kernel_amplitudes': kernel_amplitudes, 'kernel_sharpness': kernel_sharpness}
    _L0_attn_all = _L0_attn_setup()
    _L0_attn_in = {k: v for k, v in _L0_attn_all.items() if k in ('w_in', 'kernel_offsets', 'kernel_amplitudes', 'kernel_sharpness')}
    del _L0_attn_all

    def _L0_ffn_setup():
        import jax, jax.numpy as jnp
        import numpy as np
        E = 8
        TOP_K = 2
        DIM = 512
        HID = 1024
        key = jax.random.key(seed)
        k1, k2, k3, k4, k5 = jax.random.split(key, 5)
        s = 0.02
        x = jax.random.normal(k1, (2, 1024, DIM), dtype=jnp.float32)
        Wg = jax.random.normal(k2, (DIM, E), dtype=jnp.float32) * s
        W1 = jax.random.normal(k3, (E, DIM, HID), dtype=jnp.float32) * s
        W2 = jax.random.normal(k4, (E, DIM, HID), dtype=jnp.float32) * s
        W3 = jax.random.normal(k5, (E, HID, DIM), dtype=jnp.float32) * s
        return {'x': x, 'Wg': Wg, 'W1': W1, 'W2': W2, 'W3': W3}
    _L0_ffn_all = _L0_ffn_setup()
    _L0_ffn_in = {k: v for k, v in _L0_ffn_all.items() if k in ('Wg', 'W1', 'W2', 'W3')}
    del _L0_ffn_all
    return {'x': x, 'ctx_1024': ctx_1024, 'L0_xattn_Wq': _L0_xattn_in['Wq'], 'L0_xattn_bq': _L0_xattn_in['bq'], 'L0_xattn_Wk': _L0_xattn_in['Wk'], 'L0_xattn_bk': _L0_xattn_in['bk'], 'L0_xattn_Wv': _L0_xattn_in['Wv'], 'L0_xattn_bv': _L0_xattn_in['bv'], 'L0_attn_w_in': _L0_attn_in['w_in'], 'L0_attn_kernel_offsets': _L0_attn_in['kernel_offsets'], 'L0_attn_kernel_amplitudes': _L0_attn_in['kernel_amplitudes'], 'L0_attn_kernel_sharpness': _L0_attn_in['kernel_sharpness'], 'L0_ffn_Wg': _L0_ffn_in['Wg'], 'L0_ffn_W1': _L0_ffn_in['W1'], 'L0_ffn_W2': _L0_ffn_in['W2'], 'L0_ffn_W3': _L0_ffn_in['W3']}

def reference(x, ctx_1024, L0_xattn_Wq, L0_xattn_bq, L0_xattn_Wk, L0_xattn_bk, L0_xattn_Wv, L0_xattn_bv, L0_attn_w_in, L0_attn_kernel_offsets, L0_attn_kernel_amplitudes, L0_attn_kernel_sharpness, L0_ffn_Wg, L0_ffn_W1, L0_ffn_W2, L0_ffn_W3):
    import jax
    import jax.numpy as jnp

    def _L0_xattn_ref(Q, K, V, Wq, bq, Wk, bk, Wv, bv):
        import jax, jax.numpy as jnp
        import numpy as np
        H = 16
        DK = 64
        D_MODEL = 512
        B = Q.shape[0]

        def proj(x, W, b):
            y = jnp.einsum('btd,ed->bte', x, W) + b
            return y.reshape(B, -1, H, DK).transpose(0, 2, 1, 3)
        q = proj(Q, Wq, bq)
        k = proj(K, Wk, bk)
        v = proj(V, Wv, bv)
        scores = jnp.einsum('bhqd,bhkd->bhqk', q, k) / jnp.sqrt(jnp.float32(DK))
        attn = jax.nn.softmax(scores, axis=-1)
        out = jnp.einsum('bhqk,bhkd->bhqd', attn, v)
        return out.transpose(0, 2, 1, 3).reshape(B, -1, D_MODEL)

    def _L0_attn_ref(x, w_in, kernel_offsets, kernel_amplitudes, kernel_sharpness):
        import jax, jax.numpy as jnp
        import numpy as np
        B, L, D = (2, 1024, 512)
        H, K = (16, 16)
        HD = D // H

        def tisa_bias(offsets, amplitudes, sharpness, seq_len):
            rel = jnp.arange(-(seq_len - 1), seq_len, dtype=jnp.float32)
            diff = offsets[:, :, None] - rel[None, None, :]
            scores = jnp.sum(amplitudes[:, :, None] * jnp.exp(-jnp.abs(sharpness)[:, :, None] * diff * diff), axis=1)
            i = jnp.arange(seq_len)
            idx = i[:, None] - i[None, :] + (seq_len - 1)
            return scores[:, idx]
        b, l, d = x.shape
        proj = jnp.einsum('bld,ed->ble', x, w_in)
        k_, v_, q_ = (proj[..., :d], proj[..., d:2 * d], proj[..., 2 * d:])

        def heads(t):
            return t.reshape(b, l, H, HD).transpose(0, 2, 1, 3)
        q, k, v = (heads(q_), heads(k_), heads(v_))
        bias = tisa_bias(kernel_offsets, kernel_amplitudes, kernel_sharpness, l)
        scale = 1.0 / np.sqrt(HD).astype(np.float32)
        logits = jnp.einsum('bhld,bhmd->bhlm', q, k) * scale + bias[None]
        attn = jax.nn.softmax(logits, axis=-1)
        out = jnp.einsum('bhlm,bhmd->bhld', attn, v)
        return out.transpose(0, 2, 1, 3).reshape(b, l, d)

    def _L0_ffn_ref(x, Wg, W1, W2, W3):
        import jax, jax.numpy as jnp
        import numpy as np
        E = 8
        TOP_K = 2
        DIM = 512
        HID = 1024
        B, T, C = x.shape
        xf = x.reshape(-1, C)
        logits = xf @ Wg
        top_w, top_i = jax.lax.top_k(logits, TOP_K)
        top_w = jax.nn.softmax(top_w, axis=-1)
        one_hot = jax.nn.one_hot(top_i, E, dtype=xf.dtype)
        combine = jnp.einsum('nk,nke->ne', top_w, one_hot)
        h = jnp.einsum('nc,ech->enh', xf, W1)
        g = jnp.einsum('nc,ech->enh', xf, W2)
        y = jnp.einsum('enh,ehc->enc', jax.nn.silu(h) * g, W3)
        out = jnp.einsum('enc,ne->nc', y, combine)
        return out.reshape(B, T, C)
    x = x + _L0_xattn_ref(_layernorm(x, axis=-1), ctx_1024, ctx_1024, L0_xattn_Wq, L0_xattn_bq, L0_xattn_Wk, L0_xattn_bk, L0_xattn_Wv, L0_xattn_bv)
    x = x + _L0_attn_ref(_layernorm(x, axis=-1), L0_attn_w_in, L0_attn_kernel_offsets, L0_attn_kernel_amplitudes, L0_attn_kernel_sharpness)
    x = x + _L0_ffn_ref(_layernorm(x, axis=-1), L0_ffn_Wg, L0_ffn_W1, L0_ffn_W2, L0_ffn_W3)
    return x

_drawn_inputs = setup_inputs


def setup_inputs(seed=0):
    import zlib

    import numpy as np

    out = dict(_drawn_inputs(seed))
    spreads = {}
    factors = {'L0_xattn_bq': 6.398,
     'L0_xattn_bk': 64.0,
     'L0_attn_kernel_offsets': 63.53,
     'L0_attn_kernel_amplitudes': 64.0,
     'L0_attn_kernel_sharpness': 64.0}
    for name, (base, spread) in spreads.items():
        noise = np.random.default_rng([zlib.crc32(name.encode()), seed]).standard_normal(out[name].shape)
        drawn = base * np.exp(spread * noise) if base else spread * noise
        out[name] = jnp.asarray(drawn.astype(out[name].dtype))
    for name, factor in factors.items():
        out[name] = (out[name] * factor).astype(out[name].dtype)
    return out
```

```python
from contextlib import ExitStack

import concourse.bass as bass
from concourse import mybir

ALU = mybir.AluOpType
ACT = mybir.ActivationFunctionType
F16 = mybir.dt.float16
F32 = mybir.dt.float32
I32 = mybir.dt.int32
AX = mybir.AxisListType.X

P = 128
D = 512
DT = D // P
T = 256
S = 25088
CH = 512
NCH = S // CH
HC = CH // 2
NB = 8
DK = 64
W_SCALE = 16.0
Q_SCALE = 4.0
P_SCALE = 4096.0
LOGIT_SCALE = 1.0 / (W_SCALE * Q_SCALE * DK ** 0.5)
N_START = 1e30
EPS = 1e-5
H2 = 16
HD = D // H2
K2 = 16
E = 8
HID = 1024
PIECE = 256
NPC = HID // PIECE
NJ = E * NPC
FW_SCALE = 32.0
HH_SCALE = 64.0


def exists(c, n, count=NCH):
    return not isinstance(c, int) or 0 <= c + n < count


def after(c, n, least=0):
    return not isinstance(c, int) or c + n >= least


def back(c, u, lag, per=NB):
    return (c, u - lag) if u >= lag else (c - 1, u - lag + per)


def layer(nc, x, ctxt, wq, bq, wk, bk, wv, bv, w_in, offs, amps, shrp, wg, w1, w2, w3, out):
    with ExitStack() as ctx:
        def sb(name, shape, dt, stack=ctx):
            return stack.enter_context(nc.sbuf_tensor(name, shape, dt))

        def psum(name):
            return ctx.enter_context(nc.psum_tensor(name, [P, 2, 512], F32))

        def sem(name):
            return ctx.enter_context(nc.semaphore(name))

        tisa_dram = nc.dram_tensor("tisa_scores", (H2, 2, T), F32, kind="Internal")

        ident = sb("ident", [P, P], F32)
        x_sb = sb("x_sb", [P, 2, D], F32)
        xb = sb("xb", [P, 2, D], F32)
        xn = sb("xn", [P, 2, D], F32)
        xnT = sb("xnT", [P, DT, T], F32)
        stream = sb("stream", [P, 2, D], F32)
        bn6 = sb("bn6", [P, 2, 6], F32)
        mv = sb("mv", [P, 2, 2], F32)
        rstd = sb("rstd", [P, 2], F32)
        bvb = sb("bvb", [P, D], F32)
        bq_sb = sb("bq_sb", [P, DT], F32)
        bk_sb = sb("bk_sb", [P, DT], F32)
        bk_s = sb("bk_s", [P, DT], F32)
        o_acc = sb("o_acc", [P, NB, 2, DK], F32)
        l_acc = sb("l_acc", [P, 2 * NB], F32)
        nmax = [sb(f"nmax{i}", [P, 2 * NB], F32) for i in range(2)]
        lsum = [sb(f"lsum{i}", [P, 2 * NB], F32) for i in range(2)]
        dmax = sb("dmax", [P, 2 * NB], F32)
        alpha = sb("alpha", [P, 2 * NB], F32)
        cmax = sb("cmax", [P, 4, 2], F32)
        tisa = sb("tisa", [P, H2, 3, P], F32)
        tsm = sb("tsm", [P, 3, 2], F32)
        nabs = sb("nabs", [P, 2], F32)
        tsel = sb("tsel", [P, 2, H2], F32)

        cross = ExitStack()
        ctx_f = [sb(f"ctx_f{i}", [P, DT, CH], F32, cross) for i in range(2)]
        ctx_s = [[sb(f"ctx_s{i}{k}", [P, DT, CH], F16, cross) for k in range(2)] for i in range(2)]
        wk_s = [sb(f"wk_s{k}", [P, DT, D], F16, cross) for k in range(2)]
        wv_s = [sb(f"wv_s{k}", [P, DT, D], F16, cross) for k in range(2)]
        q_s = [sb(f"q_s{k}", [P, NB, T], F16, cross) for k in range(2)]
        prob = sb("prob", [P, 4, 2 * HC], F32, cross)
        pt_s = [sb(f"pt_s{k}", [P, 4, 512], F16, cross) for k in range(2)]
        setup = ExitStack()
        w_f = [sb(f"w_f{i}", [P, DT, D], F32, setup) for i in range(3)]
        q_f = sb("q_f", [P, DT, T], F32, setup)
        rel = sb("rel", [P, 2 * T], F32, setup)
        reli = sb("reli", [P, 2 * T], I32, setup)
        setup.close()
        k_s = [sb(f"k_s{i}", [P, NB, CH], F16, cross) for i in range(2)]
        v_s = [[sb(f"v_s{i}{k}", [P, 4, D], F16, cross) for k in range(2)] for i in range(2)]
        cross.close()
        w_in_sb = sb("w_in_sb", [P, DT, 3 * D], F32)
        kT = sb("kT", [P, DT, T], F32)
        qT = sb("qT", [P, DT, T], F32)
        v2 = sb("v2", [P, 2, D], F32)
        logit = sb("logit", [P, 2, 2 * T], F32)
        prob2 = sb("prob2", [P, 2, 2 * T], F32)
        pT2 = sb("pT2", [P, 2, 512], F32)
        nmax2 = sb("nmax2", [P, 2, 2], F32)
        lsum2 = sb("lsum2", [P, 2, H2], F32)
        wg_sb = sb("wg_sb", [P, DT, E], F32)
        gate = sb("gate", [P, 12, 2, E], F32)
        gone = sb("gone", [P, 8, 2], F32)
        comb = sb("comb", [P, 2 * E], F32)
        x_s = [sb(f"x_s{k}", [P, DT, T], F16) for k in range(2)]
        wst = sb("wst", [P, 4, 3, 1024], F32)
        wsp = [sb(f"wsp{k}", [P, 2, 3, 1024], F16) for k in range(2)]
        act_sb = sb("act_sb", [P, 2, T], F32)
        hh = sb("hh", [P, 2, T], F32)
        hh_s = [sb(f"hh_s{k}", [P, 4, T], F16) for k in range(2)]

        ps_proj, ps_s, ps_t, ps_o = psum("ps_proj"), psum("ps_s"), psum("ps_t"), psum("ps_o")

        x_loaded, w_loaded, small_loaded = sem("x_loaded"), sem("w_loaded"), sem("small_loaded")
        ctx_loaded = [sem("ctx_loaded0"), sem("ctx_loaded1")]
        tisa_stored, tisa_loaded, w_in_loaded = sem("tisa_stored"), sem("tisa_loaded"), sem("w_in_loaded")
        piece_loaded, out_stored = [sem(f"piece_loaded{i}") for i in range(4)], sem("out_stored")
        pool_step, ident_ready, sel_ready = sem("pool_step"), sem("ident_ready"), sem("sel_ready")
        dve_step, act_step = sem("dve_step"), sem("act_step")
        rel_ready, tisa_arg, tisa_exp = sem("rel_ready"), sem("tisa_arg"), sem("tisa_exp")
        tisa_summed, tisa_out = sem("tisa_summed"), sem("tisa_out")
        var_ready, root_done = sem("var_ready"), sem("root_done")
        ln_done, ln_turned, xT_ready = sem("ln_done"), sem("ln_turned"), sem("xT_ready")
        q_done, q_ready, w_high, w_split = sem("q_done"), sem("q_ready"), sem("w_high"), sem("w_split")
        state_ready = sem("state_ready")
        ctx_high, ctx_low = sem("ctx_high"), sem("ctx_low")
        proj_done, proj_high, proj_low = sem("proj_done"), sem("proj_high"), sem("proj_low")
        s_done, cmax_done, nmax_done, exp_done = sem("s_done"), sem("cmax_done"), sem("nmax_done"), sem("exp_done")
        t_done, pt_high, pt_low, pv_done = sem("t_done"), sem("pt_high"), sem("pt_low"), sem("pv_done")
        dmax_done, alpha_done, scaled, added = sem("dmax_done"), sem("alpha_done"), sem("scaled"), sem("added")
        l_step = sem("l_step")
        stream_ready = sem("stream_ready")
        qkv_done, k2_ready, q2_ready, v2_ready = sem("qkv_done"), sem("k2_ready"), sem("q2_ready"), sem("v2_ready")
        s2_done, logit_done, nmax2_done, exp2_done = sem("s2_done"), sem("logit_done"), sem("nmax2_done"), sem("exp2_done")
        t2_done, pt2_ready, pv2_done = sem("t2_done"), sem("pt2_ready"), sem("pv2_done")
        gate_done, gate_diff, gate_exp, x_high, x_split = sem("gate_done"), sem("gate_diff"), sem("gate_exp"), sem("x_high"), sem("x_split")
        piece_high, piece_low = sem("piece_high"), sem("piece_low")
        hg_done, silu_done, hh_done, hh_high, hh_low = sem("hg_done"), sem("silu_done"), sem("hh_done"), sem("hh_high"), sem("hh_low")
        y_done, combined = sem("y_done"), sem("combined")

        CROSS_PV = NB * NCH

        block = ctx.enter_context(nc.Block())

        def cross_steps(eng, step):
            for c in (-1, 0, 1):
                step(c, c % 2)
            with eng.Fori(2, NCH - 3, 2) as r:
                step(r, 0)
                step(r + 1, 1)
            for c in range(NCH - 3, NCH + 1):
                step(c, c % 2)

        def expert_steps(eng, step):
            step(0)
            step(1)
            with eng.Fori(2, E - 1, 1) as r:
                step(r)
            step(E - 1)
            step(E)

        @block.sync
        def _(sp):
            sp.dma_start(x_sb[:, :, :], x.rearrange("a (t r) d -> t (a r) d", r=2)).then_inc(x_loaded, 16)
            sp.dma_start(w_f[0][:, :, :], wq).then_inc(w_loaded, 16)
            sp.dma_start(w_f[1][:, :, :], wk).then_inc(w_loaded, 16)
            sp.dma_start(ctx_f[0][:, :, :], ctxt[0]).then_inc(ctx_loaded[0], 16)
            sp.dma_start(w_f[2][:, :, :], wv).then_inc(w_loaded, 16)
            sp.dma_start(ctx_f[1][:, :, :], ctxt[1]).then_inc(ctx_loaded[1], 16)

            sp.wait_ge(tisa_out, 1)
            sp.dma_start(tisa_dram.ap().rearrange("h o m -> h (o m)"), reli[0:H2, :].bitcast(F32)).then_inc(tisa_stored, 16)

            def load_chunk(k, odd):
                sp.wait_ge(ctx_high, DT * (k - 1))
                sp.wait_ge(ctx_low, DT * (k - 1))
                sp.dma_start(ctx_f[odd][:, :, :], ctxt[bass.ds(k, 1)].rearrange("a p t c -> p (a t) c")
                             if not isinstance(k, int) else ctxt[k]).then_inc(ctx_loaded[odd], 16)

            with sp.Fori(2, NCH - 1, 2) as k:
                load_chunk(k, 0)
                load_chunk(k + 1, 1)
            load_chunk(NCH - 1, (NCH - 1) % 2)
            sp.wait_ge(tisa_stored, 16)
            for i, (odd, m) in enumerate(((0, 0), (1, 0), (0, 1))):
                diagonal = bass.AP(tisa_dram, odd * T + m, [[1, P], [2 * T, H2], [1, P]])
                sp.dma_start(tisa[:, :, i, :], diagonal).then_inc(tisa_loaded, 16)
            sp.wait_ge(pv_done, CROSS_PV)
            sp.wait_ge(scaled, 2 * NCH)
            sp.wait_ge(added, 2 * NCH)
            sp.dma_start(w_in_sb[:, :, :], w_in).then_inc(w_in_loaded, 16)
            sp.dma_start(wg_sb[:, :, :], wg).then_inc(w_in_loaded, 16)

            def load_piece(j, i):
                for n, w in enumerate((w1, w2, w3)):
                    src = w[j] if isinstance(j, int) else w[bass.ds(j, 1)].rearrange("a p c -> p (a c)")
                    sp.dma_start(wst[:, i, n, :], src).then_inc(piece_loaded[i], 16)

            for i in range(4):
                load_piece(i, i)
            with sp.Fori(4, NJ - 3, 4) as j:
                for i in range(4):
                    sp.wait_ge(piece_low, 3 * (j + (i - 3)))
                    load_piece(j + i, i)
            sp.wait_ge(combined, 2 * E)
            sp.dma_start(out.rearrange("a (t r) d -> t (a r) d", r=2), stream[:, :, :]).then_inc(out_stored, 16)
            sp.wait_ge(out_stored, 16)

        @block.gpsimd
        def _(pool):
            pool.dma_start(bq_sb[:, :], bq).then_inc(small_loaded, 16)
            pool.dma_start(bk_sb[:, :], bk).then_inc(small_loaded, 16)
            pool.dma_start(bvb[:, :], bv.partition_broadcast(P)).then_inc(small_loaded, 16)
            pool.dma_start(tsm[:, 0, :], offs).then_inc(small_loaded, 16)
            pool.dma_start(tsm[:, 1, :], amps).then_inc(small_loaded, 16)
            pool.dma_start(tsm[:, 2, :], shrp).then_inc(small_loaded, 16)
            pool.memset(ident[:, :], 0.0).then_inc(pool_step, 1)
            pool.memset(tsel[:, :, :], 1.0).then_inc(pool_step, 1)
            pool.iota(reli[:, :].rearrange("p (o m) -> p o m", o=2), pattern=[[1, 2], [2, T]], base=-(T - 1),
                      channel_multiplier=0).then_inc(rel_ready, 1)
            pool.wait_ge(pool_step, 2)
            pool.affine_select(out=ident[:, :], in_=ident[:, :], compare_op=ALU.not_equal, fill=1.0, base=0,
                               pattern=[[-1, P]], channel_multiplier=1).then_inc(ident_ready, 1)
            pool.affine_select(out=tsel[:, :, :], in_=tsel[:, :, :], compare_op=ALU.is_ge, fill=0.0, base=0,
                               pattern=[[P, 2], [-K2, H2]], channel_multiplier=1).then_inc(pool_step, 1)
            pool.wait_ge(pool_step, 3)
            pool.affine_select(out=tsel[:, :, :], in_=tsel[:, :, :], compare_op=ALU.is_ge, fill=0.0, base=K2 - 1,
                               pattern=[[-P, 2], [K2, H2]], channel_multiplier=-1).then_inc(sel_ready, 1)

            def ctx_lows(k, odd, pieces):
                for t in pieces:
                    if t == 0:
                        pool.wait_ge(ctx_loaded[odd], 8 * k + (16 - 8 * odd))
                        if after(k, -2):
                            pool.wait_ge(proj_done, NB * (k - 1))
                    pool.wait_ge(ctx_high, DT * k + t + 1)
                    pool.tensor_tensor(out=ctx_s[odd][1][:, t, :], in0=ctx_f[odd][:, t, :],
                                       in1=ctx_s[odd][0][:, t, :], op=ALU.subtract).then_inc(ctx_low, 1)

            def rescale(c, half, odd):
                n = 2 * c + half
                cols = slice(NB * half, NB * half + NB)
                pool.wait_ge(alpha_done, n + 1)
                if after(c, -1):
                    pool.wait_ge(added, n - 1)
                else:
                    pool.wait_ge(state_ready, 1)
                acc = o_acc[:, 4 * half:4 * half + 4, :, :].rearrange("p u r d -> p (u r) d")
                pool.tensor_tensor(out=l_acc[:, cols], in0=l_acc[:, cols], in1=alpha[:, cols],
                                   op=ALU.mult).then_inc(l_step, 1)
                pool.tensor_tensor(out=acc, in0=acc, in1=alpha[:, cols].unsqueeze(2).to_broadcast([P, NB, DK]),
                                   op=ALU.mult)
                pool.wait_ge(l_step, n + 1)
                pool.tensor_tensor(out=l_acc[:, cols], in0=l_acc[:, cols], in1=lsum[odd][:, cols],
                                   op=ALU.add).then_inc(scaled, 1)

            def step(c, odd):
                for u in range(NB):
                    if exists(c, 2) and u % 2 == 0:
                        k = c + 2
                        ctx_lows(k, odd, (u // 2,))
                    if exists(c, -1) and u == 1:
                        rescale(c - 1, 1, 1 - odd)
                    if exists(c, 0) and u == 5:
                        rescale(c, 0, odd)

            ctx_lows(0, 0, range(DT))
            cross_steps(pool, step)

        @block.scalar
        def _(act):
            def root(i):
                act.wait_ge(var_ready, i + 1)
                act.activation(rstd[:, :], rstd[:, :], ACT.Sqrt).then_inc(root_done, 1)

            root(0)
            for i, w_s in ((1, wk_s), (2, wv_s)):
                act.wait_ge(w_loaded, 48)
                act.activation(w_s[0][:, :, :], w_f[i][:, :, :], ACT.Copy, scale=W_SCALE).then_inc(w_high, 1)

            def ctx_highs(k, odd, pieces):
                for t in pieces:
                    if t == 0:
                        act.wait_ge(ctx_loaded[odd], 8 * k + (16 - 8 * odd))
                    act.activation(ctx_s[odd][0][:, t, :], ctx_f[odd][:, t, :], ACT.Copy).then_inc(ctx_high, 1)

            def proj_highs(c, g, odd):
                act.wait_ge(proj_done, NB * c + g + 1)
                ps = ps_proj[:, g % 2, :]
                if g < 4:
                    act.activation(k_s[odd][0:64, 2 * g, :], ps[0:64, :], ACT.Identity, bias=bk_s[0:64, g:g + 1])
                    act.activation(k_s[odd][64:128, 2 * g + 1, :], ps[64:128, :], ACT.Identity,
                                   bias=bk_s[64:128, g:g + 1]).then_inc(proj_high, 1)
                else:
                    act.activation(v_s[odd][0][:, g - 4, :], ps, ACT.Copy).then_inc(proj_high, 1)

            def alphas(c, half):
                n = 2 * c + half
                cols = slice(NB * half, NB * half + NB)
                act.wait_ge(dmax_done, n + 1)
                if after(c, -1):
                    act.wait_ge(scaled, n - 1)
                act.activation(alpha[:, cols], dmax[:, cols], ACT.Exp).then_inc(alpha_done, 1)

            def step(c, odd):
                for u in range(NB):
                    pc, pg = (c, NB - 1) if u == 0 else (c + 1, u - 1)
                    if exists(pc, 0):
                        proj_highs(pc, pg, odd if u == 0 else 1 - odd)
                    tc, tu = back(c, u, 3)
                    if exists(tc, 0):
                        act.wait_ge(t_done, NB * tc + tu + 1)
                        act.activation(pt_s[0][:, tu % 4, :], ps_t[:, tu % 2, :], ACT.Copy,
                                       scale=P_SCALE).then_inc(pt_high, 1)
                    if exists(c, 0):
                        act.wait_ge(nmax_done, NB * c + u + 1)
                        if u % 4 == 0 and after(c, -2):
                            act.wait_ge(scaled, 2 * (c - 2) + u // 4 + 1)
                        for r in range(2):
                            col = 2 * u + r
                            ins = act.activation(prob[:, u % 4, r * HC:(r + 1) * HC], ps_s[:, u % 2, r * HC:(r + 1) * HC],
                                                 ACT.Exp, bias=nmax[odd][:, col:col + 1], scale=LOGIT_SCALE,
                                                 accum_out=lsum[odd][:, col:col + 1])
                        ins.then_inc(exp_done, 1)
                    if exists(c, 2) and u % 2 == 0:
                        k = c + 2
                        ctx_highs(k, odd, (u // 2,))
                    if exists(c, -1) and u == 0:
                        alphas(c - 1, 1)
                    if exists(c, 0) and u == 4:
                        alphas(c, 0)

            ctx_highs(0, 0, range(DT))
            for g in range(2):
                act.wait_ge(tisa_arg, g + 1)
                act.activation(q_f[:, 2 * g:2 * g + 2, :], q_f[:, 2 * g:2 * g + 2, :], ACT.Exp).then_inc(tisa_exp, 1)
            cross_steps(act, step)

            root(1)
            act.wait_ge(qkv_done, 1)
            act.activation(kT[:, :, :].rearrange("p t c -> p (t c)"),
                           ps_proj[:, :, :].rearrange("p b c -> p (b c)"), ACT.Copy).then_inc(k2_ready, 1)
            act.wait_ge(qkv_done, 3)
            act.activation(v2[:, :, :], ps_o[:, :, :], ACT.Copy).then_inc(v2_ready, 1)

            def copy_turned(h):
                act.wait_ge(t2_done, h + 1)
                if h >= 2:
                    act.wait_ge(pv2_done, h - 1)
                act.activation(pT2[:, h % 2, :], ps_t[:, h % 2, :], ACT.Copy).then_inc(pt2_ready, 1)

            for h in range(H2):
                act.wait_ge(nmax2_done, h + 1)
                if h >= 2:
                    act.wait_ge(t2_done, h - 1)
                for r in range(2):
                    ins = act.activation(prob2[:, h % 2, r * T:(r + 1) * T], logit[:, h % 2, r * T:(r + 1) * T], ACT.Exp,
                                         bias=nmax2[:, h % 2, r:r + 1], accum_out=lsum2[:, r, h:h + 1])
                ins.then_inc(exp2_done, 1)
                if h >= 1:
                    copy_turned(h - 1)
            copy_turned(H2 - 1)
            root(2)

            def piece_highs(j, i, parts):
                for n in parts:
                    if n == 0:
                        act.wait_ge(piece_loaded[i], 12 * j + (48 - 12 * i))
                    if n == 2 and after(j, -2):
                        act.wait_ge(y_done, 2 * (j - 1))
                    act.activation(wsp[0][:, i % 2, n, :], wst[:, i, n, :], ACT.Copy, scale=FW_SCALE).then_inc(piece_high, 1)

            piece_highs(0, 0, range(3))
            act.wait_ge(xT_ready, 6)
            act.activation(x_s[0][:, :, :], xnT[:, :, :], ACT.Copy).then_inc(x_high, 1)
            act.wait_ge(gate_diff, 1)
            act.activation(gone[:, 5, :], gone[:, 4, :], ACT.Exp).then_inc(gate_exp, 1)

            def expert(e):
                for u in range(8):
                    if exists(e, 0, E):
                        n = 8 * e + u
                        act.wait_ge(hg_done, n + 1)
                        if after(n, -2):
                            act.wait_ge(hh_done, n - 1)
                        act.activation(act_sb[:, u % 2, :], ps_proj[:, u % 2, 0:T], ACT.Silu,
                                       scale=1.0 / FW_SCALE).then_inc(silu_done, 1)
                        j, i = 4 * e + u // 2 + 1, (u // 2 + 1) % 4
                        if exists(j, 0, NJ) and not (isinstance(e, int) and j >= NJ):
                            piece_highs(j, i, (0, 1) if u % 2 == 0 else ())
                        act.wait_ge(hh_done, n + 1)
                        act.activation(hh_s[0][:, u % 4, :], hh[:, u % 2, :], ACT.Copy).then_inc(hh_high, 1)
                        if exists(j, 0, NJ):
                            piece_highs(j, i, (2,) if u % 2 == 1 else ())

            expert_steps(act, expert)

        @block.vector
        def _(dve):
            chain, roots = [0], [0]

            def link(ins):
                chain[0] += 1
                ins.then_inc(dve_step, 1)
                dve.wait_ge(dve_step, chain[0])

            def layernorm(src):
                for r in range(2):
                    ins = dve.bn_stats(bn6[:, r, :], src[:, r, :])
                link(ins)
                for r in range(2):
                    ins = dve.bn_aggr(mv[:, r, :], bn6[:, r, :])
                link(ins)
                dve.tensor_scalar(rstd[:, :], mv[:, :, 1], EPS, None, ALU.add).then_inc(var_ready, 1)
                roots[0] += 1
                dve.wait_ge(root_done, roots[0])
                link(dve.reciprocal(rstd[:, :], rstd[:, :]))
                for r in range(2):
                    ins = dve.tensor_scalar(xn[:, r, :], src[:, r, :], mv[:, r, 0:1], rstd[:, r:r + 1],
                                            ALU.subtract, ALU.mult)
                ins.then_inc(ln_done, 1)

            def turned(i):
                for r in range(2):
                    dve.wait_ge(ln_turned, 2 * i + r + 1)
                    dve.tensor_copy(xnT[:, :, r * P:(r + 1) * P],
                                    ps_t[:, r, :].rearrange("p (t c) -> p t c", t=DT)).then_inc(xT_ready, 1)

            dve.memset(nmax[1][:, :], N_START)
            dve.memset(o_acc[:, :, :, :], 0.0)
            link(dve.memset(l_acc[:, :], 0.0))
            dve.wait_ge(x_loaded, 16)
            layernorm(x_sb)
            dve.wait_ge(small_loaded, 96)
            dve.tensor_scalar(bk_s[:, :], bk_sb[:, :], W_SCALE, None, ALU.mult)
            for r in range(2):
                ins = dve.tensor_tensor(xb[:, r, :], x_sb[:, r, :], bvb[:, :], ALU.add)
            ins.then_inc(state_ready, 1)
            dve.wait_ge(rel_ready, 1)
            dve.scalar_tensor_tensor(out=nabs[:, :], in0=tsm[:, 2, :], scalar=-1.0, in1=tsm[:, 2, :], op0=ALU.mult, op1=ALU.min)
            link(dve.tensor_copy(rel[:, :], reli[:, :]))
            for g in range(2):
                d = q_f[:, 2 * g:2 * g + 2, :].rearrange("p a b -> p (a b)")
                link(dve.tensor_scalar(d, rel[:, :], tsm[:, 0, g:g + 1], None, ALU.subtract))
                dve.scalar_tensor_tensor(out=d, in0=d, scalar=nabs[:, g:g + 1], in1=d, op0=ALU.mult,
                                         op1=ALU.mult).then_inc(tisa_arg, 1)
            dve.wait_ge(sel_ready, 1)
            for g in range(2):
                ins = dve.tensor_scalar(tsel[:, g, :], tsel[:, g, :], tsm[:, 1, g:g + 1], None, ALU.mult)
            ins.then_inc(sel_ready, 1)
            turned(0)
            for i, w_s in ((1, wk_s), (2, wv_s)):
                dve.wait_ge(w_high, i)
                dve.scalar_tensor_tensor(out=w_s[1][:, :, :], in0=w_f[i][:, :, :], scalar=W_SCALE, in1=w_s[0][:, :, :],
                                         op0=ALU.mult, op1=ALU.subtract).then_inc(w_split, 1)
            dve.wait_ge(tisa_summed, 1)
            dve.tensor_copy(reli[0:H2, :].bitcast(F32), ps_s[0:H2, 0, :]).then_inc(tisa_out, 1)
            dve.wait_ge(q_done, 1)
            for t in range(DT):
                ins = dve.tensor_scalar(q_f[:, t, :], ps_proj[:, t // 2, (t % 2) * T:(t % 2 + 1) * T], bq_sb[:, t:t + 1],
                                        Q_SCALE, ALU.add, ALU.mult)
            link(ins)
            halves = ((0, 64), (64, 128))
            for b, (a0, a1) in enumerate(halves):
                for z0, z1 in halves:
                    ins = dve.tensor_copy(q_s[0][z0:z1, b::2, :], q_f[a0:a1, :, :])
            link(ins)
            for b, (a0, a1) in enumerate(halves):
                for z0, z1 in halves:
                    ins = dve.tensor_tensor(q_s[1][z0:z1, b::2, :], q_f[a0:a1, :, :], q_s[0][a0:a1, b::2, :], ALU.subtract)
            ins.then_inc(q_ready, 1)

            def step(c, odd):
                for u in range(NB):
                    if exists(c, 0):
                        dve.wait_ge(s_done, NB * c + u + 1)
                        dve.tensor_reduce(cmax[:, u % 4, :], ps_s[:, u % 2, :].rearrange("p (r k) -> p r k", r=2), AX,
                                          ALU.max).then_inc(cmax_done, 1)
                        dve.wait_ge(cmax_done, NB * c + u + 1)
                        if u == 0 and after(c, -1):
                            dve.wait_ge(dmax_done, 2 * c - 1)
                        if u == 4 and after(c, -1):
                            dve.wait_ge(dmax_done, 2 * c)
                        dve.scalar_tensor_tensor(out=nmax[odd][:, 2 * u:2 * u + 2], in0=cmax[:, u % 4, :], scalar=-LOGIT_SCALE,
                                                 in1=nmax[1 - odd][:, 2 * u:2 * u + 2], op0=ALU.mult,
                                                 op1=ALU.min).then_inc(nmax_done, 1)
                    pc, g = (c, NB - 1) if u == 0 else (c + 1, u - 1)
                    if exists(pc, 0):
                        po = odd if u == 0 else 1 - odd
                        ps = ps_proj[:, g % 2, :]
                        dve.wait_ge(proj_high, NB * pc + g + 1)
                        if g < 4:
                            for b, (a0, a1), (z0, z1) in ((0, halves[0], halves[1]), (1, halves[1], halves[0])):
                                ins = dve.scalar_tensor_tensor(out=k_s[po][z0:z1, 2 * g + b, :], in0=ps[a0:a1, :],
                                                               scalar=bk_s[a0:a1, g:g + 1], in1=k_s[po][a0:a1, 2 * g + b, :],
                                                               op0=ALU.add, op1=ALU.subtract)
                        else:
                            ins = dve.tensor_tensor(v_s[po][1][:, g - 4, :], ps, v_s[po][0][:, g - 4, :], ALU.subtract)
                        ins.then_inc(proj_low, 1)
                    tc, tu = back(c, u, 3)
                    if exists(tc, 0):
                        dve.wait_ge(pt_high, NB * tc + tu + 1)
                        dve.scalar_tensor_tensor(out=pt_s[1][:, tu % 4, :], in0=ps_t[:, tu % 2, :], scalar=P_SCALE,
                                                 in1=pt_s[0][:, tu % 4, :], op0=ALU.mult, op1=ALU.subtract).then_inc(pt_low, 1)
                    for half, (dc, dodd) in ((1, (c - 1, 1 - odd)), (0, (c, odd))):
                        if u == (0 if half else 4) and exists(dc, 0):
                            cols = slice(NB * half, NB * half + NB)
                            n = 2 * dc + half
                            dve.wait_ge(nmax_done, NB * dc + 4 * half + 4)
                            if after(dc, -1):
                                dve.wait_ge(alpha_done, n - 1)
                            dve.tensor_tensor(dmax[:, cols], nmax[dodd][:, cols], nmax[1 - dodd][:, cols],
                                              ALU.subtract).then_inc(dmax_done, 1)
                    if u in (0, 4) and exists(c, -1):
                        half, n = u // 4, 2 * (c - 1) + u // 4
                        dve.wait_ge(pv_done, NB * (c - 1) + 4 * half + 4)
                        dve.wait_ge(scaled, n + 1)
                        acc = o_acc[:, 4 * half:4 * half + 4, :, :].rearrange("p u r d -> p (u r d)")
                        dve.tensor_tensor(acc, acc, ps_o[:, half, :], ALU.add).then_inc(added, 1)

            cross_steps(dve, step)

            dve.wait_ge(scaled, 2 * NCH)
            dve.wait_ge(added, 2 * NCH)
            link(dve.reciprocal(l_acc[:, :], l_acc[:, :]))
            acc3 = o_acc[:, :, :, :].rearrange("p u r d -> p (u r) d")
            link(dve.tensor_tensor(acc3, acc3, l_acc[:, :].unsqueeze(2).to_broadcast([P, 2 * NB, DK]), ALU.mult))
            for r in range(2):
                ins = dve.scalar_tensor_tensor(out=stream[:, r, :].rearrange("p (u d) -> p u d", u=NB),
                                               in0=o_acc[:, :, r, :], scalar=1.0 / (P_SCALE * W_SCALE),
                                               in1=xb[:, r, :].rearrange("p (u d) -> p u d", u=NB), op0=ALU.mult, op1=ALU.add)
            link(ins)
            layernorm(stream)
            turned(1)
            dve.wait_ge(qkv_done, 2)
            dve.tensor_copy(qT[:, :, :].rearrange("p t c -> p (t c)"),
                            ps_s[:, :, :].rearrange("p b c -> p (b c)")).then_inc(q2_ready, 1)
            dve.wait_ge(tisa_loaded, 48)
            for h in range(H2):
                dve.wait_ge(s2_done, h + 1)
                if h >= 2:
                    dve.wait_ge(exp2_done, h - 1)
                bias = bass.AP(tisa, h * 3 * P + 2 * P - 1, [[H2 * 3 * P, P], [P, 2], [-1, 2 * P]])
                dve.scalar_tensor_tensor(out=logit[:, h % 2, :].rearrange("p (r k) -> p r k", r=2),
                                         in0=ps_s[:, h % 2, :].rearrange("p (r k) -> p r k", r=2),
                                         scalar=float(HD) ** -0.5, in1=bias, op0=ALU.mult, op1=ALU.add).then_inc(logit_done, 1)
                dve.wait_ge(logit_done, h + 1)
                dve.tensor_reduce(nmax2[:, h % 2, :], logit[:, h % 2, :].rearrange("p (r k) -> p r k", r=2), AX, ALU.max,
                                  negate=True).then_inc(nmax2_done, 1)
            dve.wait_ge(exp2_done, H2)
            link(dve.reciprocal(lsum2[:, :, :], lsum2[:, :, :]))
            dve.wait_ge(pv2_done, H2)
            for r in range(2):
                ins = dve.tensor_tensor(xn[:, r, :].rearrange("p (h d) -> p h d", h=H2),
                                        ps_proj[:, r, :].rearrange("p (h d) -> p h d", h=H2),
                                        lsum2[:, r, :].unsqueeze(2).to_broadcast([P, H2, HD]), ALU.mult)
            link(ins)
            link(dve.tensor_tensor(stream[:, :, :], stream[:, :, :], xn[:, :, :], ALU.add))
            layernorm(stream)
            turned(2)

            def piece_lows(j, i, parts):
                for n in parts:
                    dve.wait_ge(piece_high, 3 * j + n + 1)
                    dve.scalar_tensor_tensor(out=wsp[1][:, i % 2, n, :], in0=wst[:, i, n, :], scalar=FW_SCALE,
                                             in1=wsp[0][:, i % 2, n, :], op0=ALU.mult, op1=ALU.subtract).then_inc(piece_low, 1)

            piece_lows(0, 0, range(3))
            dve.wait_ge(x_high, 1)
            dve.tensor_tensor(x_s[1][:, :, :], xnT[:, :, :], x_s[0][:, :, :], ALU.subtract).then_inc(x_split, 1)
            dve.wait_ge(gate_done, 1)
            g0, rank, eq, first, rest, eq2, second = (gate[:, i, :, :] for i in range(7))
            m1, m2, c1, c2, diff, ex, den, wt1 = (gone[:, i, :] for i in range(8))

            def spread(v):
                return v.unsqueeze(2).to_broadcast([P, 2, E])

            dve.tensor_copy(g0, ps_s[:, 0, 0:2 * E].rearrange("p (r e) -> p r e", r=2))
            for e in range(E):
                ins = dve.memset(gate[:, 1, :, e:e + 1], float(E - e))
            link(ins)
            link(dve.tensor_reduce(m1, g0, AX, ALU.max))
            link(dve.tensor_tensor(eq, g0, spread(m1), ALU.is_equal))
            link(dve.tensor_tensor(eq, eq, rank, ALU.mult))
            link(dve.tensor_reduce(c1, eq, AX, ALU.max))
            link(dve.tensor_tensor(first, eq, spread(c1), ALU.is_equal))
            link(dve.scalar_tensor_tensor(out=rest, in0=first, scalar=-1e30, in1=g0, op0=ALU.mult, op1=ALU.add))
            link(dve.tensor_reduce(m2, rest, AX, ALU.max))
            link(dve.tensor_tensor(eq2, rest, spread(m2), ALU.is_equal))
            link(dve.tensor_tensor(eq2, eq2, rank, ALU.mult))
            link(dve.tensor_reduce(c2, eq2, AX, ALU.max))
            link(dve.tensor_tensor(second, eq2, spread(c2), ALU.is_equal))
            dve.tensor_tensor(diff, m2, m1, ALU.subtract).then_inc(gate_diff, 1)
            dve.wait_ge(gate_exp, 1)
            link(dve.tensor_scalar(den, ex, 1.0, None, ALU.add))
            link(dve.reciprocal(den, den))
            link(dve.tensor_scalar(wt1, den, 1.0 / (FW_SCALE * HH_SCALE), None, ALU.mult))
            link(dve.tensor_tensor(ex, ex, wt1, ALU.mult))
            link(dve.tensor_tensor(first, first, spread(wt1), ALU.mult))
            link(dve.tensor_tensor(second, second, spread(ex), ALU.mult))
            link(dve.tensor_tensor(comb[:, :].rearrange("p (r e) -> p r e", r=2), first, second, ALU.add))

            def expert(e):
                for u in range(8):
                    if exists(e, 0, E):
                        n = 8 * e + u
                        dve.wait_ge(silu_done, n + 1)
                        if after(n, -2):
                            dve.wait_ge(hh_low, n - 1)
                        dve.scalar_tensor_tensor(out=hh[:, u % 2, :], in0=ps_proj[:, u % 2, T:2 * T], scalar=HH_SCALE / FW_SCALE,
                                                 in1=act_sb[:, u % 2, :], op0=ALU.mult, op1=ALU.mult).then_inc(hh_done, 1)
                        j, i = 4 * e + u // 2 + 1, (u // 2 + 1) % 4
                        if exists(j, 0, NJ):
                            piece_lows(j, i, (0, 1) if u % 2 == 0 else ())
                        dve.wait_ge(hh_high, n + 1)
                        dve.tensor_tensor(hh_s[1][:, u % 4, :], hh[:, u % 2, :], hh_s[0][:, u % 4, :],
                                          ALU.subtract).then_inc(hh_low, 1)
                        if exists(j, 0, NJ):
                            piece_lows(j, i, (2,) if u % 2 == 1 else ())
                    if u == 1 and exists(e, -1, E):
                        dve.wait_ge(y_done, 8 * e)
                        for r in range(2):
                            if after(e, -2):
                                dve.wait_ge(combined, 2 * (e - 2) + r + 1)
                            col = e + (E * r - 1)
                            wt = comb[:, col:col + 1] if isinstance(e, int) else comb[:, bass.ds(col, 1)]
                            dve.scalar_tensor_tensor(out=stream[:, r, :], in0=ps_o[:, r, :], scalar=wt, in1=stream[:, r, :],
                                                     op0=ALU.mult, op1=ALU.add).then_inc(combined, 1)

            expert_steps(dve, expert)

        @block.tensor
        def _(pe):
            THREE = ((0, 0), (1, 0), (0, 1))

            def turn(i):
                pe.wait_ge(ln_done, i + 1)
                for r in range(2):
                    for t in range(DT):
                        ins = pe.transpose(ps_t[:, r, t * P:(t + 1) * P], xn[:, r, t * P:(t + 1) * P], ident[:, :])
                    ins.then_inc(ln_turned, 1)

            pe.wait_ge(ident_ready, 1)
            turn(0)
            pe.wait_ge(sel_ready, 2)
            pe.wait_ge(tisa_exp, 2)
            for g in range(2):
                ins = pe.matmul(ps_s[0:H2, 0, :], tsel[:, g, :], q_f[:, 2 * g:2 * g + 2, :].rearrange("p a b -> p (a b)"),
                                start=(g == 0), stop=(g == 1))
            ins.then_inc(tisa_summed, 1)
            pe.wait_ge(w_loaded, 48)
            pe.wait_ge(xT_ready, 2)
            for e in range(DT):
                for t in range(DT):
                    ins = pe.matmul(ps_proj[:, e // 2, (e % 2) * T:(e % 2 + 1) * T], w_f[0][:, t, e * P:(e + 1) * P],
                                    xnT[:, t, :], start=(t == 0), stop=(t == DT - 1))
            ins.then_inc(q_done, 1)
            pe.wait_ge(w_split, 2)
            pe.wait_ge(q_ready, 1)
            pe.wait_ge(tisa_stored, 16)

            def step(c, odd):
                for u in range(NB):
                    if exists(c, 0):
                        if u % 2 == 0:
                            pe.wait_ge(proj_low, NB * c + u // 2 + 1)
                        if u >= 2 or after(c, -1):
                            pe.wait_ge(exp_done, NB * c + u - 1)
                        for r in range(2):
                            for part in range(2):
                                ins = pe.matmul(ps_s[:, u % 2, r * HC:(r + 1) * HC], q_s[part][:, u, r * P:(r + 1) * P],
                                                k_s[odd][:, u, r * HC:(r + 1) * HC], start=(part == 0), stop=(part == 1))
                        ins.then_inc(s_done, 1)
                    if exists(c, 1):
                        if u == 0:
                            pe.wait_ge(ctx_low, DT * (c + 2))
                        if u >= 2 or after(c, 0):
                            pe.wait_ge(proj_low, NB * c + NB + u - 1)
                        cs = ctx_s[1 - odd]
                        for t in range(DT):
                            for n, (a, b) in enumerate(THREE):
                                if u < 4:
                                    lhsT, rhs = wk_s[a][:, t, u * P:(u + 1) * P], cs[b][:, t, :]
                                else:
                                    lhsT, rhs = cs[b][:, t, (u - 4) * P:(u - 3) * P], wv_s[a][:, t, :]
                                ins = pe.matmul(ps_proj[:, u % 2, :], lhsT, rhs, start=(t == 0 and n == 0),
                                                stop=(t == DT - 1 and n == 2))
                        ins.then_inc(proj_done, 1)
                    tc, tu = back(c, u, 2)
                    if exists(tc, 0):
                        pe.wait_ge(exp_done, NB * tc + tu + 1)
                        if tu >= 2 or after(tc, -1):
                            pe.wait_ge(pt_low, NB * tc + tu - 1)
                        for i in range(4):
                            ins = pe.transpose(ps_t[:, tu % 2, i * P:(i + 1) * P], prob[:, tu % 4, i * P:(i + 1) * P], ident[:, :])
                        ins.then_inc(t_done, 1)
                    vc, vu = back(c, u, 4)
                    if exists(vc, 0):
                        vodd = odd if u >= 4 else 1 - odd
                        pe.wait_ge(pt_low, NB * vc + vu + 1)
                        if vu == 0:
                            pe.wait_ge(proj_low, NB * vc + NB)
                        if vu % 4 == 0 and after(vc, -1):
                            pe.wait_ge(added, 2 * vc + vu // 4 - 1)
                        for r in range(2):
                            col = (vu % 4) * 2 * DK + r * DK
                            for i in range(2):
                                tile = 2 * r + i
                                for n, (a, b) in enumerate(THREE):
                                    ins = pe.matmul(ps_o[:, vu // 4, col:col + DK], pt_s[a][:, vu % 4, tile * P:(tile + 1) * P],
                                                    v_s[vodd][b][:, tile, vu * DK:(vu + 1) * DK],
                                                    start=(i == 0 and n == 0), stop=(i == 1 and n == 2))
                        ins.then_inc(pv_done, 1)

            cross_steps(pe, step)

            turn(1)
            pe.wait_ge(xT_ready, 4)
            pe.wait_ge(w_in_loaded, 32)
            for base, ps in ((0, ps_proj), (2 * D, ps_s)):
                for e in range(DT):
                    for t in range(DT):
                        ins = pe.matmul(ps[:, e // 2, (e % 2) * T:(e % 2 + 1) * T], w_in_sb[:, t, base + e * P:base + (e + 1) * P],
                                        xnT[:, t, :], start=(t == 0), stop=(t == DT - 1))
                ins.then_inc(qkv_done, 1)
            for r in range(2):
                for t in range(DT):
                    ins = pe.matmul(ps_o[:, r, :], xnT[:, t, r * P:(r + 1) * P], w_in_sb[:, t, D:2 * D],
                                    start=(t == 0), stop=(t == DT - 1))
            ins.then_inc(qkv_done, 1)
            pe.wait_ge(k2_ready, 1)
            pe.wait_ge(q2_ready, 1)
            for h in range(H2 + 2):
                if h < H2:
                    if h >= 2:
                        pe.wait_ge(logit_done, h - 1)
                    rows = slice(HD * (h % 4), HD * (h % 4 + 1))
                    for r in range(2):
                        ins = pe.matmul(ps_s[:, h % 2, r * T:(r + 1) * T], qT[rows, h // 4, r * P:(r + 1) * P],
                                        kT[rows, h // 4, :], start=True, stop=True)
                    ins.then_inc(s2_done, 1)
                if 1 <= h <= H2:
                    g = h - 1
                    pe.wait_ge(exp2_done, g + 1)
                    if g >= 2:
                        pe.wait_ge(pt2_ready, g - 1)
                    for i in range(4):
                        ins = pe.transpose(ps_t[:, g % 2, i * P:(i + 1) * P], prob2[:, g % 2, i * P:(i + 1) * P], ident[:, :])
                    ins.then_inc(t2_done, 1)
                if h >= 2:
                    g = h - 2
                    pe.wait_ge(pt2_ready, g + 1)
                    if g == 0:
                        pe.wait_ge(v2_ready, 1)
                    for r in range(2):
                        for s in range(2):
                            ins = pe.matmul(ps_proj[:, r, g * HD:(g + 1) * HD], pT2[:, g % 2, (2 * r + s) * P:(2 * r + s + 1) * P],
                                            v2[:, s, g * HD:(g + 1) * HD], start=(s == 0), stop=(s == 1))
                    ins.then_inc(pv2_done, 1)

            turn(2)
            pe.wait_ge(xT_ready, 6)
            for r in range(2):
                for t in range(DT):
                    ins = pe.matmul(ps_s[:, 0, r * E:(r + 1) * E], xnT[:, t, r * P:(r + 1) * P], wg_sb[:, t, :],
                                    start=(t == 0), stop=(t == DT - 1))
            ins.then_inc(gate_done, 1)
            pe.wait_ge(x_split, 1)

            def expert(e):
                for u in range(8):
                    if exists(e, 0, E):
                        n = 8 * e + u
                        if u % 2 == 0:
                            pe.wait_ge(piece_low, 3 * (4 * e + u // 2) + 2)
                        if after(n, -2):
                            pe.wait_ge(hh_done, n - 1)
                        for m in range(2):
                            for t in range(DT):
                                for k, (a, b) in enumerate(THREE):
                                    col = t * PIECE + (u % 2) * P
                                    ins = pe.matmul(ps_proj[:, u % 2, m * T:(m + 1) * T], wsp[a][:, (u // 2) % 2, m, col:col + P],
                                                    x_s[b][:, t, :], start=(t == 0 and k == 0), stop=(t == DT - 1 and k == 2))
                        ins.then_inc(hg_done, 1)
                    ye, yu = back(e, u, 2)
                    if exists(ye, 0, E):
                        n = 8 * ye + yu
                        pe.wait_ge(hh_low, n + 1)
                        if yu % 2 == 0:
                            pe.wait_ge(piece_low, 3 * (4 * ye + yu // 2) + 3)
                        if yu == 0 and after(ye, -1):
                            pe.wait_ge(combined, 2 * ye)
                        for r in range(2):
                            for k, (a, b) in enumerate(THREE):
                                ins = pe.matmul(ps_o[:, r, :], hh_s[a][:, yu % 4, r * P:(r + 1) * P],
                                                wsp[b][:, (yu // 2) % 2, 2, (yu % 2) * D:(yu % 2 + 1) * D],
                                                start=(yu == 0 and k == 0), stop=(yu == 7 and k == 2))
                        ins.then_inc(y_done, 1)

            expert_steps(pe, expert)


def kernel(x, ctx_1024, L0_xattn_Wq, L0_xattn_bq, L0_xattn_Wk, L0_xattn_bk, L0_xattn_Wv, L0_xattn_bv, L0_attn_w_in,
           L0_attn_kernel_offsets, L0_attn_kernel_amplitudes, L0_attn_kernel_sharpness, L0_ffn_Wg, L0_ffn_W1, L0_ffn_W2,
           L0_ffn_W3):
    import numpy as np
    import concourse.bacc as bacc
    from concourse.bass_utils import run_bass_kernel_spmd

    def rows_on_partitions(w):
        return w.reshape(DT, P, -1).transpose(1, 0, 2)

    arrays = {
        "x": x,
        "ctxt": ctx_1024.reshape(NCH, HC, 2, DT, P).transpose(0, 4, 3, 2, 1).reshape(NCH, P, DT, CH),
        "wq": rows_on_partitions(L0_xattn_Wq.T), "bq": L0_xattn_bq.reshape(DT, P).T,
        "wk": rows_on_partitions(L0_xattn_Wk.T), "bk": L0_xattn_bk.reshape(DT, P).T,
        "wv": rows_on_partitions(L0_xattn_Wv.T), "bv": L0_xattn_bv,
        "w_in": rows_on_partitions(L0_attn_w_in.T),
        "offs": L0_attn_kernel_offsets.reshape(2, P).T,
        "amps": L0_attn_kernel_amplitudes.reshape(2, P).T,
        "shrp": L0_attn_kernel_sharpness.reshape(2, P).T,
        "wg": rows_on_partitions(L0_ffn_Wg),
        "w1": L0_ffn_W1.reshape(E, DT, P, NPC, PIECE).transpose(0, 3, 2, 1, 4).reshape(NJ, P, DT * PIECE),
        "w2": L0_ffn_W2.reshape(E, DT, P, NPC, PIECE).transpose(0, 3, 2, 1, 4).reshape(NJ, P, DT * PIECE),
        "w3": L0_ffn_W3.reshape(E, NPC, PIECE // P, P, D).transpose(0, 1, 3, 2, 4).reshape(NJ, P, PIECE // P * D),
    }
    nc = bacc.Bacc("TRN2", target_bir_lowering=False, num_devices=1)
    data, aps = {}, []
    for name, a in arrays.items():
        data[name + "_dram"] = np.ascontiguousarray(a)
        aps.append(nc.dram_tensor(name + "_dram", a.shape, F32, kind="ExternalInput").ap())
    aps.append(nc.dram_tensor("out_dram", (1, T, D), F32, kind="ExternalOutput").ap())
    layer(nc, *aps)
    return run_bass_kernel_spmd(nc, [data], core_ids=[0]).results[0]["out_dram"]
```

```python
from contextlib import ExitStack

import concourse.bass as bass
from concourse import mybir

ALU = mybir.AluOpType
ACT = mybir.ActivationFunctionType
F16 = mybir.dt.float16
F32 = mybir.dt.float32
I32 = mybir.dt.int32
AX = mybir.AxisListType.X

P = 128
D = 512
DT = D // P
T = 256
S = 25088
CH = 512
NCH = S // CH
HC = CH // 2
NB = 8
DK = 64
W_SCALE = 16.0
Q_SCALE = 4.0
P_SCALE = 4096.0
A_SCALE = 16.0
LOGIT_SCALE = 1.0 / (W_SCALE * Q_SCALE * DK ** 0.5)
N_START = 1e30
TURN_LAG = 2
PV_LAG = 5
EPS = 1e-5
H2 = 16
HD = D // H2
K2 = 16
E = 8
HID = 1024
PIECE = 256
NPC = HID // PIECE
NJ = E * NPC
FW_SCALE = 32.0
HH_SCALE = 64.0


def exists(c, n, count=NCH):
    return not isinstance(c, int) or 0 <= c + n < count


def after(c, n, least=0):
    return not isinstance(c, int) or c + n >= least


def back(c, u, lag, per=NB):
    return (c, u - lag) if u >= lag else (c - 1, u - lag + per)


def layer(nc, x, ctxt, wq, wk, wv, bv, cols, w_in, wg, w1, w2, w3, out):
    with ExitStack() as ctx:
        def sb(name, shape, dt, stack=ctx):
            return stack.enter_context(nc.sbuf_tensor(name, shape, dt))

        def psum(name, banks):
            return ctx.enter_context(nc.psum_tensor(name, [P, banks, 512], F32))

        def sem(name):
            return ctx.enter_context(nc.semaphore(name))

        tisa_dram = nc.dram_tensor("tisa_scores", (H2, 2, T), F32, kind="Internal")

        ident = sb("ident", [P, P], F32)
        xb = sb("xb", [P, 2, D], F32)
        xn = sb("xn", [P, 2, D], F32)
        xnT = sb("xnT", [P, DT, T], F32)
        stream = sb("stream", [P, 2, D], F32)
        bn6 = sb("bn6", [P, 2, 6], F32)
        mv = sb("mv", [P, 2, 2], F32)
        rstd = sb("rstd", [P, 2], F32)
        bvb = sb("bvb", [P, D], F32)
        cols_sb = sb("cols_sb", [P, 2 * DT + 6], F32)
        bq_sb, bk_sb = cols_sb[:, 0:DT], cols_sb[:, DT:2 * DT]
        off_sb, amp_sb, shrp_sb = (cols_sb[:, 2 * DT + 2 * i:2 * DT + 2 * i + 2] for i in range(3))
        bk_s = sb("bk_s", [P, DT], F32)
        o_acc = sb("o_acc", [P, NB, 2, DK], F32)
        l_acc = sb("l_acc", [P, 2 * NB], F32)
        nmax = [sb(f"nmax{i}", [P, 2 * NB], F32) for i in range(2)]
        lsum = [sb(f"lsum{i}", [P, 2 * NB], F32) for i in range(2)]
        dmax = sb("dmax", [P, 2 * NB], F32)
        alpha = sb("alpha", [P, 2 * NB], F32)
        cmax = sb("cmax", [P, 4, 2], F32)
        w_in_sb = sb("w_in_sb", [P, DT, 3 * D], F32)
        nabs = sb("nabs", [P, 2], F32)
        tsel = sb("tsel", [P, 2, H2], F32)

        cross = ExitStack()
        ctx_f = [sb(f"ctx_f{i}", [P, DT, CH], F32, cross) for i in range(2)]
        ctx_s = [[sb(f"ctx_s{i}{k}", [P, DT, CH], F16, cross) for k in range(2)] for i in range(2)]
        wk_s = [sb(f"wk_s{k}", [P, DT, D], F16, cross) for k in range(2)]
        wv_s = [sb(f"wv_s{k}", [P, DT, D], F16, cross) for k in range(2)]
        q_s = [sb(f"q_s{k}", [P, NB, T], F16, cross) for k in range(2)]
        k_s = [sb(f"k_s{i}", [P, NB, CH], F16, cross) for i in range(2)]
        v_s = [[sb(f"v_s{i}{k}", [P, 4, D], F16, cross) for k in range(2)] for i in range(2)]
        setup = ExitStack()
        w_f = [sb(f"w_f{i}", [P, DT, D], F32, setup) for i in range(3)]
        q_f = sb("q_f", [P, DT, T], F32, setup)
        tisa_e = sb("tisa_e", [P, 2, 2 * T], F32, setup)
        rel = sb("rel", [P, 2 * T], F32, setup)
        reli = sb("reli", [P, 2 * T], I32, setup)
        setup.close()
        prob = sb("prob", [P, 4, 2 * HC], F32, cross)
        p_s = sb("p_s", [P, 4, 2, 2 * HC], F16, cross)
        pt_s = sb("pt_s", [P, NB, 2, 4, P], F16, cross)
        cross.close()
        tisa = sb("tisa", [P, H2, 3, P], F32)
        kT_s = [sb(f"kT_s{k}", [P, DT * T], F16) for k in range(2)]
        qT_s = [sb(f"qT_s{k}", [P, DT * T], F16) for k in range(2)]
        v2_s = [sb(f"v2_s{k}", [P, 2 * D], F16) for k in range(2)]
        logit = sb("logit", [P, 2, 2 * T], F32)
        prob2 = sb("prob2", [P, 2, 2 * T], F32)
        pT2_s = [sb(f"pT2_s{k}", [P, 4, 512], F16) for k in range(2)]
        nmax2 = sb("nmax2", [P, 2, 2], F32)
        lsum2 = sb("lsum2", [P, 2, H2], F32)
        wg_sb = sb("wg_sb", [P, DT, E], F32)
        wg_s = [sb(f"wg_s{k}", [P, DT, E], F16) for k in range(2)]
        gate = sb("gate", [P, 12, 2, E], F32)
        gone = sb("gone", [P, 8, 2], F32)
        comb = sb("comb", [P, 2 * E], F32)
        x_s = [sb(f"x_s{k}", [P, DT, T], F16) for k in range(2)]
        wst = sb("wst", [P, 4, 3, 1024], F32)
        wsp = [sb(f"wsp{k}", [P, 2, 3, 1024], F16) for k in range(2)]
        act_sb = sb("act_sb", [P, 2, T], F32)
        hh = sb("hh", [P, 2, T], F32)
        hh_s = [sb(f"hh_s{k}", [P, 4, T], F16) for k in range(2)]

        ps_proj, ps_s, ps_o = psum("ps_proj", 4), psum("ps_s", 2), psum("ps_o", 2)

        turned_p = [sem(f"turned_p{u}") for u in range(NB)]
        wg_high, wg_low = sem("wg_high"), sem("wg_low")
        may_turn = sem("may_turn")
        wk_loaded, wv_loaded = sem("wk_loaded"), sem("wv_loaded")
        x_loaded, wq_loaded, small_loaded = sem("x_loaded"), sem("wq_loaded"), sem("small_loaded")
        ctx_loaded = [sem("ctx_loaded0"), sem("ctx_loaded1")]
        tisa_stored, tisa_loaded, w_in_loaded = sem("tisa_stored"), sem("tisa_loaded"), sem("w_in_loaded")
        piece_loaded, out_stored = [sem(f"piece_loaded{i}") for i in range(4)], sem("out_stored")
        pool_step, ident_ready, sel_ready = sem("pool_step"), sem("ident_ready"), sem("sel_ready")
        dve_step, act_step = sem("dve_step"), sem("act_step")
        rel_ready, tisa_arg, tisa_exp = sem("rel_ready"), sem("tisa_arg"), sem("tisa_exp")
        tisa_summed, tisa_out = sem("tisa_summed"), sem("tisa_out")
        var_ready, root_done = sem("var_ready"), sem("root_done")
        ln_done, ln_turned, xT_ready = sem("ln_done"), sem("ln_turned"), sem("xT_ready")
        q_done, q_ready, w_high, w_split = sem("q_done"), sem("q_ready"), sem("w_high"), sem("w_split")
        state_ready = sem("state_ready")
        ctx_high, ctx_low = sem("ctx_high"), sem("ctx_low")
        proj_done, proj_high, proj_low = sem("proj_done"), sem("proj_high"), sem("proj_low")
        s_done, cmax_done, nmax_done, exp_done = sem("s_done"), sem("cmax_done"), sem("nmax_done"), sem("exp_done")
        p_high, p_low, pv_done = sem("p_high"), sem("p_low"), sem("pv_done")
        dmax_done, alpha_done, scaled, added = sem("dmax_done"), sem("alpha_done"), sem("scaled"), sem("added")
        l_step = sem("l_step")
        stream_ready = sem("stream_ready")
        qkv_done, qkv_high, qkv_low = sem("qkv_done"), sem("qkv_high"), sem("qkv_low")
        s2_done, logit_done, nmax2_done, exp2_done = sem("s2_done"), sem("logit_done"), sem("nmax2_done"), sem("exp2_done")
        t2_done, pt2_high, pt2_low, pv2_done = sem("t2_done"), sem("pt2_high"), sem("pt2_low"), sem("pv2_done")
        gate_done, gate_diff, gate_exp, x_high, x_split = sem("gate_done"), sem("gate_diff"), sem("gate_exp"), sem("x_high"), sem("x_split")
        piece_high, piece_low = sem("piece_high"), sem("piece_low")
        hg_done, silu_done, hh_done, hh_high, hh_low = sem("hg_done"), sem("silu_done"), sem("hh_done"), sem("hh_high"), sem("hh_low")
        y_done, combined = sem("y_done"), sem("combined")

        LOOP_END = NCH - 5
        CROSS_PV = NB * NCH

        KQV = ((kT_s, ps_proj[:, 0:2, :].rearrange("p b c -> p (b c)")), (qT_s, ps_proj[:, 2:4, :].rearrange("p b c -> p (b c)")),
               (v2_s, ps_o[:, :, :].rearrange("p b c -> p (b c)")))

        block = ctx.enter_context(nc.Block())

        def cross_steps(eng, step):
            for c in (-1, 0, 1):
                step(c, c % 2)
            with eng.Fori(2, LOOP_END - 1, 2) as r:
                step(r, 0)
                step(r + 1, 1)
            for c in range(LOOP_END, NCH + 1):
                step(c, c % 2)

        def expert_steps(eng, step):
            step(0)
            step(1)
            with eng.Fori(2, E - 1, 1) as r:
                step(r)
            step(E - 1)
            step(E)

        @block.sync
        def _(sp):
            def load_chunk(k, odd):
                src = ctxt[k] if isinstance(k, int) else ctxt[bass.ds(k, 1)].rearrange("a p t c -> p (a t) c")
                sp.dma_start(ctx_f[odd][:, :, :], src).then_inc(ctx_loaded[odd], 16)

            sp.dma_start(stream[:, :, :], x.rearrange("a (t r) d -> t (a r) d", r=2)).then_inc(x_loaded, 16)
            sp.dma_start(w_f[1][:, :, :], wk).then_inc(wk_loaded, 16)
            load_chunk(0, 0)
            sp.dma_start(w_f[2][:, :, :], wv).then_inc(wv_loaded, 16)
            sp.dma_start(w_f[0][:, :, :], wq).then_inc(wq_loaded, 16)
            load_chunk(1, 1)
            sp.wait_ge(ctx_low, DT)
            load_chunk(2, 0)
            sp.dma_start(w_in_sb[:, :, :], w_in).then_inc(w_in_loaded, 16)
            sp.wait_ge(tisa_out, 1)
            sp.dma_start(tisa_dram.ap().rearrange("h o m -> h (o m)"), reli[0:H2, :].bitcast(F32)).then_inc(tisa_stored, 16)

            def step(c, odd):
                if exists(c, 4):
                    sp.wait_ge(ctx_high, DT * (c + 3))
                    sp.wait_ge(ctx_low, DT * (c + 3))
                    load_chunk(c + 4, odd)

            cross_steps(sp, step)
            sp.wait_ge(pv_done, CROSS_PV)
            sp.wait_ge(scaled, 2 * NCH)
            sp.wait_ge(added, 2 * NCH)
            def load_piece(j, i):
                for n, w in enumerate((w1, w2, w3)):
                    src = w[j] if isinstance(j, int) else w[bass.ds(j, 1)].rearrange("a p c -> p (a c)")
                    sp.dma_start(wst[:, i, n, :], src).then_inc(piece_loaded[i], 16)

            load_piece(0, 0)
            sp.wait_ge(tisa_stored, 16)
            for i, (odd, m) in enumerate(((0, 0), (1, 0), (0, 1))):
                diagonal = bass.AP(tisa_dram, odd * T + m, [[1, P], [2 * T, H2], [1, P]])
                sp.dma_start(tisa[:, :, i, :], diagonal).then_inc(tisa_loaded, 16)
            sp.dma_start(wg_sb[:, :, :], wg).then_inc(w_in_loaded, 16)

            for i in range(1, 4):
                load_piece(i, i)
            with sp.Fori(4, NJ - 3, 4) as j:
                for i in range(4):
                    sp.wait_ge(piece_low, 3 * (j + (i - 3)))
                    load_piece(j + i, i)
            sp.wait_ge(combined, 2 * E)
            sp.dma_start(out.rearrange("a (t r) d -> t (a r) d", r=2), stream[:, :, :]).then_inc(out_stored, 16)
            sp.wait_ge(out_stored, 16)

        @block.gpsimd
        def _(pool):
            pool.memset(ident[:, :], 0.0).then_inc(pool_step, 1)
            pool.memset(tsel[:, :, :], 1.0).then_inc(pool_step, 1)
            pool.iota(reli[:, :].rearrange("p (o m) -> p o m", o=2), pattern=[[1, 2], [2, T]], base=-(T - 1),
                      channel_multiplier=0).then_inc(rel_ready, 1)
            pool.wait_ge(pool_step, 2)
            pool.affine_select(out=ident[:, :], in_=ident[:, :], compare_op=ALU.not_equal, fill=1.0, base=0,
                               pattern=[[-1, P]], channel_multiplier=1).then_inc(ident_ready, 1)
            pool.affine_select(out=tsel[:, :, :], in_=tsel[:, :, :], compare_op=ALU.is_ge, fill=0.0, base=0,
                               pattern=[[P, 2], [-K2, H2]], channel_multiplier=1).then_inc(pool_step, 1)
            pool.wait_ge(pool_step, 3)
            pool.affine_select(out=tsel[:, :, :], in_=tsel[:, :, :], compare_op=ALU.is_ge, fill=0.0, base=K2 - 1,
                               pattern=[[-P, 2], [K2, H2]], channel_multiplier=-1).then_inc(sel_ready, 1)

            def ctx_lows(k, odd, pieces):
                for t in pieces:
                    if t == 0:
                        pool.wait_ge(ctx_loaded[odd], 8 * k + (16 - 8 * odd))
                        if after(k, -2):
                            pool.wait_ge(proj_done, NB * (k - 1))
                    pool.wait_ge(ctx_high, DT * k + t + 1)
                    pool.tensor_tensor(out=ctx_s[odd][1][:, t, :], in0=ctx_f[odd][:, t, :],
                                       in1=ctx_s[odd][0][:, t, :], op=ALU.subtract).then_inc(ctx_low, 1)

            def rescale(c, half, odd):
                n = 2 * c + half
                cols = slice(NB * half, NB * half + NB)
                pool.wait_ge(alpha_done, n + 1)
                if after(c, -1):
                    pool.wait_ge(added, n - 1)
                else:
                    pool.wait_ge(state_ready, 1)
                acc = o_acc[:, 4 * half:4 * half + 4, :, :].rearrange("p u r d -> p (u r) d")
                pool.tensor_tensor(out=l_acc[:, cols], in0=l_acc[:, cols], in1=alpha[:, cols],
                                   op=ALU.mult).then_inc(l_step, 1)
                pool.tensor_tensor(out=acc, in0=acc, in1=alpha[:, cols].unsqueeze(2).to_broadcast([P, NB, DK]),
                                   op=ALU.mult)
                pool.wait_ge(l_step, n + 1)
                pool.tensor_tensor(out=l_acc[:, cols], in0=l_acc[:, cols], in1=lsum[odd][:, cols],
                                   op=ALU.add).then_inc(scaled, 1)

            def step(c, odd):
                for u in range(NB):
                    if exists(c, 2) and u % 2 == 0:
                        k = c + 2
                        ctx_lows(k, odd, (u // 2,))
                    if exists(c, -1) and u == 1:
                        rescale(c - 1, 1, 1 - odd)
                    if exists(c, 0) and u == 5:
                        rescale(c, 0, odd)

            ctx_lows(0, 0, range(DT))
            cross_steps(pool, step)

        @block.scalar
        def _(act):
            def root(i):
                act.wait_ge(var_ready, i + 1)
                act.activation(rstd[:, :], rstd[:, :], ACT.Sqrt).then_inc(root_done, 1)

            act.dma_start(cols_sb[:, :], cols).then_inc(small_loaded, 16)
            act.dma_start(bvb[:, :], bv.partition_broadcast(P)).then_inc(small_loaded, 16)
            root(0)
            def ctx_highs(k, odd, pieces):
                for t in pieces:
                    if t == 0:
                        act.wait_ge(ctx_loaded[odd], 8 * k + (16 - 8 * odd))
                    act.activation(ctx_s[odd][0][:, t, :], ctx_f[odd][:, t, :], ACT.Copy).then_inc(ctx_high, 1)

            def proj_highs(c, g, odd):
                act.wait_ge(proj_done, NB * c + g + 1)
                ps = ps_proj[:, g % 4, :]
                if g < 4:
                    act.activation(k_s[odd][0:64, 2 * g, :], ps[0:64, :], ACT.Identity, bias=bk_s[0:64, g:g + 1])
                    act.activation(k_s[odd][64:128, 2 * g + 1, :], ps[64:128, :], ACT.Identity,
                                   bias=bk_s[64:128, g:g + 1]).then_inc(proj_high, 1)
                else:
                    act.activation(v_s[odd][0][:, g - 4, :], ps, ACT.Copy).then_inc(proj_high, 1)

            def alphas(c, half):
                n = 2 * c + half
                cols = slice(NB * half, NB * half + NB)
                act.wait_ge(dmax_done, n + 1)
                if after(c, -1):
                    act.wait_ge(scaled, n - 1)
                act.activation(alpha[:, cols], dmax[:, cols], ACT.Exp).then_inc(alpha_done, 1)

            def step(c, odd):
                for u in range(NB):
                    pc, pg = (c, NB - 1) if u == 0 else (c + 1, u - 1)
                    if exists(pc, 0):
                        proj_highs(pc, pg, odd if u == 0 else 1 - odd)
                    tc, tu = back(c, u, TURN_LAG)
                    if exists(tc, 0):
                        act.wait_ge(p_low, NB * tc + tu + 1)
                        if after(tc, -1):
                            act.wait_ge(pv_done, NB * (tc - 1) + tu + 1)
                        act.sem_inc(may_turn, 1)
                        act.dma_start_transpose(pt_s[:, tu, :, :, :].rearrange("p k b q -> p (k b) q"),
                                                p_s[:, tu % 4, :, :].rearrange("p k c -> p (k c)")).then_inc(turned_p[tu], 16)
                    tc, tu = back(c, u, 1)
                    if exists(tc, 0):
                        act.wait_ge(exp_done, NB * tc + tu + 1)
                        fc, fu = back(c, u, 5)
                        if exists(fc, 0):
                            act.wait_ge(turned_p[fu], 16 * fc + 16)
                        act.activation(p_s[:, tu % 4, 0, :], prob[:, tu % 4, :], ACT.Copy, scale=P_SCALE).then_inc(p_high, 1)
                    if exists(c, 0):
                        act.wait_ge(nmax_done, NB * c + u + 1)
                        if u % 4 == 0 and after(c, -2):
                            act.wait_ge(scaled, 2 * (c - 2) + u // 4 + 1)
                        for r in range(2):
                            col = 2 * u + r
                            ins = act.activation(prob[:, u % 4, r * HC:(r + 1) * HC], ps_s[:, u % 2, r * HC:(r + 1) * HC],
                                                 ACT.Exp, bias=nmax[odd][:, col:col + 1], scale=LOGIT_SCALE,
                                                 accum_out=lsum[odd][:, col:col + 1])
                        ins.then_inc(exp_done, 1)
                    if exists(c, 2) and u % 2 == 0:
                        k = c + 2
                        ctx_highs(k, odd, (u // 2,))
                    if exists(c, -1) and u == 0:
                        alphas(c - 1, 1)
                    if exists(c, 0) and u == 4:
                        alphas(c, 0)

            act.wait_ge(wk_loaded, 16)
            act.activation(wk_s[0][:, :, :], w_f[1][:, :, :], ACT.Copy, scale=W_SCALE).then_inc(w_high, 1)
            ctx_highs(0, 0, range(DT))
            for g in range(2):
                act.wait_ge(tisa_arg, g + 1)
                act.activation(tisa_e[:, g, :], tisa_e[:, g, :], ACT.Exp).then_inc(tisa_exp, 1)
            act.wait_ge(wv_loaded, 16)
            act.activation(wv_s[0][:, :, :], w_f[2][:, :, :], ACT.Copy, scale=W_SCALE).then_inc(w_high, 1)
            cross_steps(act, step)

            root(1)
            def high_of(i):
                act.wait_ge(qkv_done, i + 1)
                act.activation(KQV[i][0][0][:, :], KQV[i][1], ACT.Copy, scale=A_SCALE).then_inc(qkv_high, 1)

            def piece_highs(j, i, parts):
                for n in parts:
                    if n == 0:
                        act.wait_ge(piece_loaded[i], 12 * j + (48 - 12 * i))
                    if n == 2 and after(j, -2):
                        act.wait_ge(y_done, 2 * (j - 1))
                    act.activation(wsp[0][:, i % 2, n, :], wst[:, i, n, :], ACT.Copy, scale=FW_SCALE).then_inc(piece_high, 1)

            piece_highs(0, 0, range(3))
            high_of(0)
            act.wait_ge(w_in_loaded, 32)
            act.activation(wg_s[0][:, :, :], wg_sb[:, :, :], ACT.Copy, scale=FW_SCALE).then_inc(wg_high, 1)
            high_of(1)

            def copy_turned(h):
                act.wait_ge(t2_done, h + 1)
                if h >= 4:
                    act.wait_ge(pv2_done, h - 3)
                act.activation(pT2_s[0][:, h % 4, :], ps_proj[:, 2 + h % 2, :], ACT.Copy, scale=P_SCALE).then_inc(pt2_high, 1)

            for h in range(H2):
                act.wait_ge(nmax2_done, h + 1)
                if h >= 2:
                    act.wait_ge(t2_done, h - 1)
                for r in range(2):
                    ins = act.activation(prob2[:, h % 2, r * T:(r + 1) * T], logit[:, h % 2, r * T:(r + 1) * T], ACT.Exp,
                                         bias=nmax2[:, h % 2, r:r + 1], accum_out=lsum2[:, r, h:h + 1])
                ins.then_inc(exp2_done, 1)
                if h >= 1:
                    copy_turned(h - 1)
                if h == 1:
                    high_of(2)
            copy_turned(H2 - 1)
            root(2)

            act.wait_ge(xT_ready, 6)
            act.activation(x_s[0][:, :, :], xnT[:, :, :], ACT.Copy).then_inc(x_high, 1)

            def expert(e):
                for u in range(8):
                    if exists(e, 0, E):
                        n = 8 * e + u
                        act.wait_ge(hg_done, n + 1)
                        if after(n, -2):
                            act.wait_ge(hh_done, n - 1)
                        act.activation(act_sb[:, u % 2, :], ps_proj[:, u % 2, 0:T], ACT.Silu,
                                       scale=1.0 / FW_SCALE).then_inc(silu_done, 1)
                        j, i = 4 * e + u // 2 + 1, (u // 2 + 1) % 4
                        if exists(j, 0, NJ) and not (isinstance(e, int) and j >= NJ):
                            piece_highs(j, i, (0, 1) if u % 2 == 0 else ())
                        act.wait_ge(hh_done, n + 1)
                        act.activation(hh_s[0][:, u % 4, :], hh[:, u % 2, :], ACT.Copy).then_inc(hh_high, 1)
                        if isinstance(e, int) and e == 0 and u == 5:
                            act.wait_ge(gate_diff, 1)
                            act.activation(gone[:, 5, :], gone[:, 4, :], ACT.Exp, scale=1.0 / FW_SCALE).then_inc(gate_exp, 1)
                        if exists(j, 0, NJ):
                            piece_highs(j, i, (2,) if u % 2 == 1 else ())

            expert_steps(act, expert)

        @block.vector
        def _(dve):
            chain, roots = [0], [0]

            def link(ins):
                chain[0] += 1
                ins.then_inc(dve_step, 1)
                dve.wait_ge(dve_step, chain[0])

            def layernorm(src):
                for r in range(2):
                    ins = dve.bn_stats(bn6[:, r, :], src[:, r, :])
                link(ins)
                for r in range(2):
                    ins = dve.bn_aggr(mv[:, r, :], bn6[:, r, :])
                link(ins)
                dve.tensor_scalar(rstd[:, :], mv[:, :, 1], EPS, None, ALU.add).then_inc(var_ready, 1)
                roots[0] += 1
                dve.wait_ge(root_done, roots[0])
                link(dve.reciprocal(rstd[:, :], rstd[:, :]))
                for r in range(2):
                    dve.tensor_scalar(xn[:, r, :], src[:, r, :], mv[:, r, 0:1], rstd[:, r:r + 1],
                                      ALU.subtract, ALU.mult).then_inc(ln_done, 1)

            def turned(i):
                for r in range(2):
                    dve.wait_ge(ln_turned, 2 * i + r + 1)
                    dve.tensor_copy(xnT[:, :, r * P:(r + 1) * P],
                                    ps_s[:, r, :].rearrange("p (t c) -> p t c", t=DT)).then_inc(xT_ready, 1)

            dve.memset(nmax[1][:, :], N_START)
            dve.memset(o_acc[:, :, :, :], 0.0)
            link(dve.memset(l_acc[:, :], 0.0))
            dve.wait_ge(x_loaded, 16)
            layernorm(stream)
            dve.wait_ge(w_high, 1)
            dve.scalar_tensor_tensor(out=wk_s[1][:, :, :], in0=w_f[1][:, :, :], scalar=W_SCALE, in1=wk_s[0][:, :, :],
                                     op0=ALU.mult, op1=ALU.subtract).then_inc(w_split, 1)
            turned(0)
            dve.wait_ge(small_loaded, 32)
            dve.tensor_scalar(bk_s[:, :], bk_sb, W_SCALE, None, ALU.mult)
            for r in range(2):
                ins = dve.tensor_tensor(xb[:, r, :], stream[:, r, :], bvb[:, :], ALU.add)
            ins.then_inc(state_ready, 1)
            dve.wait_ge(rel_ready, 1)
            dve.scalar_tensor_tensor(out=nabs[:, :], in0=shrp_sb, scalar=-1.0, in1=shrp_sb, op0=ALU.mult, op1=ALU.min)
            link(dve.tensor_copy(rel[:, :], reli[:, :]))
            for g in range(2):
                d = tisa_e[:, g, :]
                link(dve.tensor_scalar(d, rel[:, :], off_sb[:, g:g + 1], None, ALU.subtract))
                dve.scalar_tensor_tensor(out=d, in0=d, scalar=nabs[:, g:g + 1], in1=d, op0=ALU.mult,
                                         op1=ALU.mult).then_inc(tisa_arg, 1)
            dve.wait_ge(sel_ready, 1)
            for g in range(2):
                ins = dve.tensor_scalar(tsel[:, g, :], tsel[:, g, :], amp_sb[:, g:g + 1], None, ALU.mult)
            ins.then_inc(sel_ready, 1)
            dve.wait_ge(w_high, 2)
            dve.scalar_tensor_tensor(out=wv_s[1][:, :, :], in0=w_f[2][:, :, :], scalar=W_SCALE, in1=wv_s[0][:, :, :],
                                     op0=ALU.mult, op1=ALU.subtract).then_inc(w_split, 1)
            halves = ((0, 64), (64, 128))

            def tisa_scores():
                dve.wait_ge(tisa_summed, 1)
                dve.tensor_copy(reli[0:H2, :].bitcast(F32), ps_s[0:H2, 0, :]).then_inc(tisa_out, 1)

            def split_q():
                dve.wait_ge(q_done, 1)
                for t in range(DT):
                    ins = dve.tensor_scalar(q_f[:, t, :], ps_o[:, t // 2, (t % 2) * T:(t % 2 + 1) * T], bq_sb[:, t:t + 1],
                                            Q_SCALE, ALU.add, ALU.mult)
                link(ins)
                for b, (a0, a1) in enumerate(halves):
                    for z0, z1 in halves:
                        ins = dve.tensor_copy(q_s[0][z0:z1, b::2, :], q_f[a0:a1, :, :])
                link(ins)
                for b, (a0, a1) in enumerate(halves):
                    for z0, z1 in halves:
                        ins = dve.tensor_tensor(q_s[1][z0:z1, b::2, :], q_f[a0:a1, :, :], q_s[0][a0:a1, b::2, :], ALU.subtract)
                ins.then_inc(q_ready, 1)

            def step(c, odd):
                for u in range(NB):
                    if exists(c, 0):
                        dve.wait_ge(s_done, NB * c + u + 1)
                        dve.tensor_reduce(cmax[:, u % 4, :], ps_s[:, u % 2, :].rearrange("p (r k) -> p r k", r=2), AX,
                                          ALU.max).then_inc(cmax_done, 1)
                        dve.wait_ge(cmax_done, NB * c + u + 1)
                        if u == 0 and after(c, -1):
                            dve.wait_ge(dmax_done, 2 * c - 1)
                        if u == 4 and after(c, -1):
                            dve.wait_ge(dmax_done, 2 * c)
                        dve.scalar_tensor_tensor(out=nmax[odd][:, 2 * u:2 * u + 2], in0=cmax[:, u % 4, :], scalar=-LOGIT_SCALE,
                                                 in1=nmax[1 - odd][:, 2 * u:2 * u + 2], op0=ALU.mult,
                                                 op1=ALU.min).then_inc(nmax_done, 1)
                    pc, g = (c, NB - 1) if u == 0 else (c + 1, u - 1)
                    if exists(pc, 0):
                        po = odd if u == 0 else 1 - odd
                        ps = ps_proj[:, g % 4, :]
                        dve.wait_ge(proj_high, NB * pc + g + 1)
                        if g < 4:
                            for b, (a0, a1), (z0, z1) in ((0, halves[0], halves[1]), (1, halves[1], halves[0])):
                                ins = dve.scalar_tensor_tensor(out=k_s[po][z0:z1, 2 * g + b, :], in0=ps[a0:a1, :],
                                                               scalar=bk_s[a0:a1, g:g + 1], in1=k_s[po][a0:a1, 2 * g + b, :],
                                                               op0=ALU.add, op1=ALU.subtract)
                        else:
                            ins = dve.tensor_tensor(v_s[po][1][:, g - 4, :], ps, v_s[po][0][:, g - 4, :], ALU.subtract)
                        ins.then_inc(proj_low, 1)
                    tc, tu = back(c, u, 1)
                    if exists(tc, 0):
                        dve.wait_ge(p_high, NB * tc + tu + 1)
                        dve.scalar_tensor_tensor(out=p_s[:, tu % 4, 1, :], in0=prob[:, tu % 4, :], scalar=P_SCALE,
                                                 in1=p_s[:, tu % 4, 0, :], op0=ALU.mult, op1=ALU.subtract).then_inc(p_low, 1)
                    for half, (dc, dodd) in ((1, (c - 1, 1 - odd)), (0, (c, odd))):
                        if u == (0 if half else 4) and exists(dc, 0):
                            cols = slice(NB * half, NB * half + NB)
                            n = 2 * dc + half
                            dve.wait_ge(nmax_done, NB * dc + 4 * half + 4)
                            if after(dc, -1):
                                dve.wait_ge(alpha_done, n - 1)
                            dve.tensor_tensor(dmax[:, cols], nmax[dodd][:, cols], nmax[1 - dodd][:, cols],
                                              ALU.subtract).then_inc(dmax_done, 1)
                    if u in (1, 5) and exists(c, -1):
                        half, n = u // 4, 2 * (c - 1) + u // 4
                        dve.wait_ge(pv_done, NB * (c - 1) + 4 * half + 4)
                        dve.wait_ge(scaled, n + 1)
                        acc = o_acc[:, 4 * half:4 * half + 4, :, :].rearrange("p u r d -> p (u r d)")
                        dve.tensor_tensor(acc, acc, ps_o[:, half, :], ALU.add).then_inc(added, 1)
                        if isinstance(c, int) and c == NCH:
                            dve.wait_ge(added, 2 * c - 1 + half)
                            if half == 0:
                                dve.wait_ge(scaled, 2 * NCH)
                                link(dve.reciprocal(l_acc[:, :], l_acc[:, :]))
                            acc3 = o_acc[:, 4 * half:4 * half + 4, :, :].rearrange("p u r d -> p (u r) d")
                            ins = dve.tensor_tensor(acc3, acc3, l_acc[:, NB * half:NB * half + NB].unsqueeze(2)
                                                    .to_broadcast([P, NB, DK]), ALU.mult)
                            if half == 1:
                                link(ins)
                    if isinstance(c, int) and c == -1 and u == 2:
                        tisa_scores()
                    if isinstance(c, int) and c == -1 and u == 4:
                        split_q()

            cross_steps(dve, step)

            for r in range(2):
                ins = dve.scalar_tensor_tensor(out=stream[:, r, :].rearrange("p (u d) -> p u d", u=NB),
                                               in0=o_acc[:, :, r, :], scalar=1.0 / (P_SCALE * W_SCALE),
                                               in1=xb[:, r, :].rearrange("p (u d) -> p u d", u=NB), op0=ALU.mult, op1=ALU.add)
            link(ins)
            layernorm(stream)
            turned(1)
            def low_of(i):
                parts, ps = KQV[i]
                dve.wait_ge(qkv_high, i + 1)
                dve.scalar_tensor_tensor(out=parts[1][:, :], in0=ps, scalar=A_SCALE, in1=parts[0][:, :], op0=ALU.mult,
                                         op1=ALU.subtract).then_inc(qkv_low, 1)

            def piece_lows(j, i, parts):
                for n in parts:
                    dve.wait_ge(piece_high, 3 * j + n + 1)
                    dve.scalar_tensor_tensor(out=wsp[1][:, i % 2, n, :], in0=wst[:, i, n, :], scalar=FW_SCALE,
                                             in1=wsp[0][:, i % 2, n, :], op0=ALU.mult, op1=ALU.subtract).then_inc(piece_low, 1)

            piece_lows(0, 0, range(3))
            low_of(0)
            dve.wait_ge(wg_high, 1)
            dve.scalar_tensor_tensor(out=wg_s[1][:, :, :], in0=wg_sb[:, :, :], scalar=FW_SCALE, in1=wg_s[0][:, :, :],
                                     op0=ALU.mult, op1=ALU.subtract).then_inc(wg_low, 1)
            low_of(1)

            def low_turned(h):
                dve.wait_ge(pt2_high, h + 1)
                dve.scalar_tensor_tensor(out=pT2_s[1][:, h % 4, :], in0=ps_proj[:, 2 + h % 2, :], scalar=P_SCALE,
                                         in1=pT2_s[0][:, h % 4, :], op0=ALU.mult, op1=ALU.subtract).then_inc(pt2_low, 1)

            dve.wait_ge(tisa_loaded, 48)
            for h in range(H2):
                dve.wait_ge(s2_done, h + 1)
                if h >= 2:
                    dve.wait_ge(exp2_done, h - 1)
                bias = bass.AP(tisa, h * 3 * P + 2 * P - 1, [[H2 * 3 * P, P], [P, 2], [-1, 2 * P]])
                dve.scalar_tensor_tensor(out=logit[:, h % 2, :].rearrange("p (r k) -> p r k", r=2),
                                         in0=ps_s[:, h % 2, :].rearrange("p (r k) -> p r k", r=2),
                                         scalar=float(HD) ** -0.5 / A_SCALE ** 2, in1=bias, op0=ALU.mult, op1=ALU.add).then_inc(logit_done, 1)
                dve.wait_ge(logit_done, h + 1)
                dve.tensor_reduce(nmax2[:, h % 2, :], logit[:, h % 2, :].rearrange("p (r k) -> p r k", r=2), AX, ALU.max,
                                  negate=True).then_inc(nmax2_done, 1)
                if h >= 2:
                    low_turned(h - 2)
                if h == 2:
                    low_of(2)
            low_turned(H2 - 2)
            dve.wait_ge(exp2_done, H2)
            link(dve.reciprocal(lsum2[:, :, :], lsum2[:, :, :]))
            low_turned(H2 - 1)
            dve.wait_ge(pv2_done, H2)
            for r in range(2):
                ins = dve.tensor_tensor(xn[:, r, :].rearrange("p (h d) -> p h d", h=H2),
                                        ps_proj[:, r, :].rearrange("p (h d) -> p h d", h=H2),
                                        lsum2[:, r, :].unsqueeze(2).to_broadcast([P, H2, HD]), ALU.mult)
            link(ins)
            link(dve.scalar_tensor_tensor(out=stream[:, :, :], in0=xn[:, :, :], scalar=1.0 / (P_SCALE * A_SCALE),
                                          in1=stream[:, :, :], op0=ALU.mult, op1=ALU.add))
            layernorm(stream)
            turned(2)

            dve.wait_ge(x_high, 1)
            dve.tensor_tensor(x_s[1][:, :, :], xnT[:, :, :], x_s[0][:, :, :], ALU.subtract).then_inc(x_split, 1)
            g0, rank, eq, first, rest, eq2, second = (gate[:, i, :, :] for i in range(7))
            m1, m2, c1, c2, diff, ex, den, wt1 = (gone[:, i, :] for i in range(8))

            def spread(v):
                return v.unsqueeze(2).to_broadcast([P, 2, E])

            def route():
                dve.wait_ge(gate_done, 1)
                dve.tensor_copy(g0, ps_s[:, 0, 0:2 * E].rearrange("p (r e) -> p r e", r=2))
                for e in range(E):
                    ins = dve.memset(gate[:, 1, :, e:e + 1], float(E - e))
                link(ins)
                link(dve.tensor_reduce(m1, g0, AX, ALU.max))
                link(dve.tensor_tensor(eq, g0, spread(m1), ALU.is_equal))
                link(dve.tensor_tensor(eq, eq, rank, ALU.mult))
                link(dve.tensor_reduce(c1, eq, AX, ALU.max))
                link(dve.tensor_tensor(first, eq, spread(c1), ALU.is_equal))
                link(dve.scalar_tensor_tensor(out=rest, in0=first, scalar=-1e30, in1=g0, op0=ALU.mult, op1=ALU.add))
                link(dve.tensor_reduce(m2, rest, AX, ALU.max))
                link(dve.tensor_tensor(eq2, rest, spread(m2), ALU.is_equal))
                link(dve.tensor_tensor(eq2, eq2, rank, ALU.mult))
                link(dve.tensor_reduce(c2, eq2, AX, ALU.max))
                link(dve.tensor_tensor(second, eq2, spread(c2), ALU.is_equal))
                dve.tensor_tensor(diff, m2, m1, ALU.subtract).then_inc(gate_diff, 1)

            def weigh():
                dve.wait_ge(gate_exp, 1)
                link(dve.tensor_scalar(den, ex, 1.0, None, ALU.add))
                link(dve.reciprocal(den, den))
                link(dve.tensor_scalar(wt1, den, 1.0 / (FW_SCALE * HH_SCALE), None, ALU.mult))
                link(dve.tensor_tensor(ex, ex, wt1, ALU.mult))
                link(dve.tensor_tensor(first, first, spread(wt1), ALU.mult))
                link(dve.tensor_tensor(second, second, spread(ex), ALU.mult))
                link(dve.tensor_tensor(comb[:, :].rearrange("p (r e) -> p r e", r=2), first, second, ALU.add))

            def expert(e):
                for u in range(8):
                    if exists(e, 0, E):
                        n = 8 * e + u
                        dve.wait_ge(silu_done, n + 1)
                        if after(n, -2):
                            dve.wait_ge(hh_low, n - 1)
                        dve.scalar_tensor_tensor(out=hh[:, u % 2, :], in0=ps_proj[:, u % 2, T:2 * T], scalar=HH_SCALE / FW_SCALE,
                                                 in1=act_sb[:, u % 2, :], op0=ALU.mult, op1=ALU.mult).then_inc(hh_done, 1)
                        j, i = 4 * e + u // 2 + 1, (u // 2 + 1) % 4
                        if exists(j, 0, NJ):
                            piece_lows(j, i, (0, 1) if u % 2 == 0 else ())
                        dve.wait_ge(hh_high, n + 1)
                        dve.tensor_tensor(hh_s[1][:, u % 4, :], hh[:, u % 2, :], hh_s[0][:, u % 4, :],
                                          ALU.subtract).then_inc(hh_low, 1)
                    if u == 1 and exists(e, -1, E):
                        dve.wait_ge(y_done, 8 * e)
                        for r in range(2):
                            if after(e, -2):
                                dve.wait_ge(combined, 2 * (e - 2) + r + 1)
                            col = e + (E * r - 1)
                            wt = comb[:, col:col + 1] if isinstance(e, int) else comb[:, bass.ds(col, 1)]
                            dve.scalar_tensor_tensor(out=stream[:, r, :], in0=ps_o[:, r, :], scalar=wt, in1=stream[:, r, :],
                                                     op0=ALU.mult, op1=ALU.add).then_inc(combined, 1)
                    if exists(e, 0, E):
                        j, i = 4 * e + u // 2 + 1, (u // 2 + 1) % 4
                        if exists(j, 0, NJ):
                            piece_lows(j, i, (2,) if u % 2 == 1 else ())
                    if isinstance(e, int) and e == 0 and u == 2:
                        route()
                    if isinstance(e, int) and e == 0 and u == 5:
                        weigh()

            expert_steps(dve, expert)

        @block.tensor
        def _(pe):
            THREE = ((0, 0), (1, 0), (0, 1))

            def turn(i):
                for r in range(2):
                    pe.wait_ge(ln_done, 2 * i + r + 1)
                    for t in range(DT):
                        ins = pe.transpose(ps_s[:, r, t * P:(t + 1) * P], xn[:, r, t * P:(t + 1) * P], ident[:, :])
                    ins.then_inc(ln_turned, 1)

            pe.wait_ge(ident_ready, 1)
            turn(0)

            def tisa_scores():
                pe.wait_ge(sel_ready, 2)
                pe.wait_ge(tisa_exp, 2)
                pe.wait_ge(xT_ready, 2)
                for g in range(2):
                    ins = pe.matmul(ps_s[0:H2, 0, :], tsel[:, g, :], tisa_e[:, g, :], start=(g == 0), stop=(g == 1))
                ins.then_inc(tisa_summed, 1)

            def project_q():
                pe.wait_ge(wq_loaded, 16)
                for e in range(DT):
                    for t in range(DT):
                        ins = pe.matmul(ps_o[:, e // 2, (e % 2) * T:(e % 2 + 1) * T], w_f[0][:, t, e * P:(e + 1) * P],
                                        xnT[:, t, :], start=(t == 0), stop=(t == DT - 1))
                ins.then_inc(q_done, 1)

            def step(c, odd):
                for u in range(NB):
                    if exists(c, 0):
                        if u % 2 == 0:
                            pe.wait_ge(proj_low, NB * c + u // 2 + 1)
                        if isinstance(c, int) and c == 0 and u == 0:
                            pe.wait_ge(q_ready, 1)
                        if u >= 2 or after(c, -1):
                            pe.wait_ge(exp_done, NB * c + u - 1)
                        for r in range(2):
                            for part in range(2):
                                ins = pe.matmul(ps_s[:, u % 2, r * HC:(r + 1) * HC], q_s[part][:, u, r * P:(r + 1) * P],
                                                k_s[odd][:, u, r * HC:(r + 1) * HC], start=(part == 0), stop=(part == 1))
                        ins.then_inc(s_done, 1)
                    vc, vu = back(c, u, PV_LAG)
                    if exists(vc, 0):
                        vodd = odd if u >= PV_LAG else 1 - odd
                        pe.wait_ge(turned_p[vu], 16 * vc + 16)
                        if vu == 0:
                            pe.wait_ge(proj_low, NB * vc + NB)
                        if vu % 4 == 0 and after(vc, -1):
                            pe.wait_ge(added, 2 * vc + vu // 4 - 1)
                        for r in range(2):
                            col = (vu % 4) * 2 * DK + r * DK
                            for i in range(2):
                                tile = 2 * r + i
                                for n, (a, b) in enumerate(THREE):
                                    ins = pe.matmul(ps_o[:, vu // 4, col:col + DK], pt_s[:, vu, a, tile, :],
                                                    v_s[vodd][b][:, tile, vu * DK:(vu + 1) * DK],
                                                    start=(i == 0 and n == 0), stop=(i == 1 and n == 2))
                        ins.then_inc(pv_done, 1)
                    if exists(c, 1):
                        if u == 0:
                            pe.wait_ge(ctx_low, DT * (c + 2))
                        if isinstance(c, int) and c == -1 and u in (0, 4):
                            pe.wait_ge(w_split, 1 + u // 4)
                        if u >= 4 or after(c, 0):
                            pe.wait_ge(proj_low, NB * c + NB + u - 3)
                        cs = ctx_s[1 - odd]
                        for t in range(DT):
                            for n, (a, b) in enumerate(THREE):
                                if u < 4:
                                    lhsT, rhs = wk_s[a][:, t, u * P:(u + 1) * P], cs[b][:, t, :]
                                else:
                                    lhsT, rhs = cs[b][:, t, (u - 4) * P:(u - 3) * P], wv_s[a][:, t, :]
                                ins = pe.matmul(ps_proj[:, u % 4, :], lhsT, rhs, start=(t == 0 and n == 0),
                                                stop=(t == DT - 1 and n == 2))
                        ins.then_inc(proj_done, 1)
                    if isinstance(c, int) and c == -1 and u == 1:
                        tisa_scores()
                    if isinstance(c, int) and c == -1 and u == 3:
                        project_q()
                    if isinstance(c, int) and c == -1 and u == NB - 1:
                        pe.wait_ge(tisa_stored, 16)
            cross_steps(pe, step)

            turn(1)
            pe.wait_ge(xT_ready, 4)
            pe.wait_ge(w_in_loaded, 16)
            for base, b in ((0, 0), (2 * D, 2)):
                for e in range(DT):
                    for t in range(DT):
                        ins = pe.matmul(ps_proj[:, b + e // 2, (e % 2) * T:(e % 2 + 1) * T],
                                        w_in_sb[:, t, base + e * P:base + (e + 1) * P], xnT[:, t, :], start=(t == 0),
                                        stop=(t == DT - 1))
                ins.then_inc(qkv_done, 1)

            def project_v(r):
                for t in range(DT):
                    ins = pe.matmul(ps_o[:, r, :], xnT[:, t, r * P:(r + 1) * P], w_in_sb[:, t, D:2 * D],
                                    start=(t == 0), stop=(t == DT - 1))
                return ins

            project_v(0)
            pe.wait_ge(qkv_low, 2)
            for h in range(H2 + 3):
                if h < H2:
                    if h >= 2:
                        pe.wait_ge(logit_done, h - 1)
                    rows, col = slice(HD * (h % 4), HD * (h % 4 + 1)), (h // 4) * T
                    for r in range(2):
                        for n, (a, b) in enumerate(THREE):
                            ins = pe.matmul(ps_s[:, h % 2, r * T:(r + 1) * T], qT_s[a][rows, col + r * P:col + (r + 1) * P],
                                            kT_s[b][rows, col:col + T], start=(n == 0), stop=(n == 2))
                    ins.then_inc(s2_done, 1)
                if h == 0:
                    project_v(1).then_inc(qkv_done, 1)
                if 1 <= h <= H2:
                    g = h - 1
                    pe.wait_ge(exp2_done, g + 1)
                    if g >= 2:
                        pe.wait_ge(pt2_low, g - 1)
                    for i in range(4):
                        ins = pe.transpose(ps_proj[:, 2 + g % 2, i * P:(i + 1) * P], prob2[:, g % 2, i * P:(i + 1) * P], ident[:, :])
                    ins.then_inc(t2_done, 1)
                if h >= 3:
                    g = h - 3
                    pe.wait_ge(pt2_low, g + 1)
                    if g == 0:
                        pe.wait_ge(qkv_low, 3)
                    for r in range(2):
                        for s in range(2):
                            for n, (a, b) in enumerate(THREE):
                                ins = pe.matmul(ps_proj[:, r, g * HD:(g + 1) * HD],
                                                pT2_s[a][:, g % 4, (2 * r + s) * P:(2 * r + s + 1) * P],
                                                v2_s[b][:, s * D + g * HD:s * D + (g + 1) * HD],
                                                start=(s == 0 and n == 0), stop=(s == 1 and n == 2))
                    ins.then_inc(pv2_done, 1)

            turn(2)
            pe.wait_ge(xT_ready, 6)
            pe.wait_ge(x_split, 1)

            def expert(e):
                for u in range(8):
                    if exists(e, 0, E):
                        n = 8 * e + u
                        if u % 2 == 0:
                            pe.wait_ge(piece_low, 3 * (4 * e + u // 2) + 2)
                        if after(n, -2):
                            pe.wait_ge(hh_done, n - 1)
                        for m in range(2):
                            for t in range(DT):
                                for k, (a, b) in enumerate(THREE):
                                    col = t * PIECE + (u % 2) * P
                                    ins = pe.matmul(ps_proj[:, u % 2, m * T:(m + 1) * T], wsp[a][:, (u // 2) % 2, m, col:col + P],
                                                    x_s[b][:, t, :], start=(t == 0 and k == 0), stop=(t == DT - 1 and k == 2))
                        ins.then_inc(hg_done, 1)
                        if isinstance(e, int) and e == 0 and u == 1:
                            pe.wait_ge(wg_low, 1)
                            for r in range(2):
                                for t in range(DT):
                                    for k, (a, b) in enumerate(THREE):
                                        ins = pe.matmul(ps_s[:, 0, r * E:(r + 1) * E], x_s[a][:, t, r * P:(r + 1) * P],
                                                        wg_s[b][:, t, :], start=(t == 0 and k == 0),
                                                        stop=(t == DT - 1 and k == 2))
                            ins.then_inc(gate_done, 1)
                    ye, yu = back(e, u, 2)
                    if exists(ye, 0, E):
                        n = 8 * ye + yu
                        pe.wait_ge(hh_low, n + 1)
                        if yu % 2 == 0:
                            pe.wait_ge(piece_low, 3 * (4 * ye + yu // 2) + 3)
                        if yu == 0 and after(ye, -1):
                            pe.wait_ge(combined, 2 * ye)
                        for r in range(2):
                            for k, (a, b) in enumerate(THREE):
                                ins = pe.matmul(ps_o[:, r, :], hh_s[a][:, yu % 4, r * P:(r + 1) * P],
                                                wsp[b][:, (yu // 2) % 2, 2, (yu % 2) * D:(yu % 2 + 1) * D],
                                                start=(yu == 0 and k == 0), stop=(yu == 7 and k == 2))
                        ins.then_inc(y_done, 1)

            expert_steps(pe, expert)


def kernel(x, ctx_1024, L0_xattn_Wq, L0_xattn_bq, L0_xattn_Wk, L0_xattn_bk, L0_xattn_Wv, L0_xattn_bv, L0_attn_w_in,
           L0_attn_kernel_offsets, L0_attn_kernel_amplitudes, L0_attn_kernel_sharpness, L0_ffn_Wg, L0_ffn_W1, L0_ffn_W2,
           L0_ffn_W3):
    import numpy as np
    import concourse.bacc as bacc
    from concourse.bass_utils import run_bass_kernel_spmd

    def rows_on_partitions(w):
        return w.reshape(DT, P, -1).transpose(1, 0, 2)

    arrays = {
        "x": x,
        "ctxt": ctx_1024.reshape(NCH, HC, 2, DT, P).transpose(0, 4, 3, 2, 1).reshape(NCH, P, DT, CH),
        "wq": rows_on_partitions(L0_xattn_Wq.T),
        "wk": rows_on_partitions(L0_xattn_Wk.T),
        "wv": rows_on_partitions(L0_xattn_Wv.T),
        "bv": L0_xattn_bv,
        "cols": np.concatenate([a.reshape(-1, P).T for a in (L0_xattn_bq, L0_xattn_bk, L0_attn_kernel_offsets,
                                                             L0_attn_kernel_amplitudes, L0_attn_kernel_sharpness)], axis=1),
        "w_in": rows_on_partitions(L0_attn_w_in.T),
        "wg": rows_on_partitions(L0_ffn_Wg),
        "w1": L0_ffn_W1.reshape(E, DT, P, NPC, PIECE).transpose(0, 3, 2, 1, 4).reshape(NJ, P, DT * PIECE),
        "w2": L0_ffn_W2.reshape(E, DT, P, NPC, PIECE).transpose(0, 3, 2, 1, 4).reshape(NJ, P, DT * PIECE),
        "w3": L0_ffn_W3.reshape(E, NPC, PIECE // P, P, D).transpose(0, 1, 3, 2, 4).reshape(NJ, P, PIECE // P * D),
    }
    nc = bacc.Bacc("TRN2", target_bir_lowering=False, num_devices=1)
    data, aps = {}, []
    for name, a in arrays.items():
        data[name + "_dram"] = np.ascontiguousarray(a)
        aps.append(nc.dram_tensor(name + "_dram", a.shape, F32, kind="ExternalInput").ap())
    aps.append(nc.dram_tensor("out_dram", (1, T, D), F32, kind="ExternalOutput").ap())
    layer(nc, *aps)
    return run_bass_kernel_spmd(nc, [data], core_ids=[0]).results[0]["out_dram"]
```
